# Optimizing a Trainium2 kernel written in Bass

```python
import numpy as np
import jax
import jax.numpy as jnp

def _softmax(x, axis=-1):
    return jax.nn.softmax(x, axis=axis)

def _gelu(x):
    return jax.nn.gelu(x, approximate=True)

def _silu(x):
    return jax.nn.silu(x)

def _sigmoid(x):
    return jax.nn.sigmoid(x)

def _layernorm(x, axis=-1, eps=1e-05):
    m = jnp.mean(x, axis=axis, keepdims=True)
    v = jnp.var(x, axis=axis, keepdims=True)
    return (x - m) / jnp.sqrt(v + eps)

def _scatter_add(tgt, idx, src, axis=0):
    return tgt.at[idx].add(src)

def _segment_sum(src, seg, n):
    return jax.ops.segment_sum(src, seg, n)
kernel_name = 'mk_gnn_preln_d4_gnn_r8_c2b613'

def setup_inputs(seed: int=0):
    np.random.seed(seed)
    _w = jnp.asarray

    def _rec_inputs():
        import jax
        import jax.numpy as jnp
        _gk = jax.random.key(seed)
        x = -8.776e-05 + 1 * jax.random.normal(jax.random.fold_in(_gk, 1), (1250, 512), jnp.float32)
        src = jax.random.randint(jax.random.fold_in(_gk, 2), (20000,), 0, 1250, jnp.int32)
        dst = jax.random.randint(jax.random.fold_in(_gk, 3), (20000,), 0, 1250, jnp.int32)
        _o = jnp.argsort(dst, stable=True)
        src = src[_o]
        dst = dst[_o]
        edge_type_2 = jax.random.randint(jax.random.fold_in(_gk, 14), (20000,), 0, 2, jnp.int32)
        edge_weight = jax.random.uniform(jax.random.fold_in(_gk, 15), (20000,), jnp.float32, 0.0, 0.0999999)
        node_vec = jax.random.uniform(jax.random.fold_in(_gk, 16), (1250,), jnp.float32, 0.0, 0.999988)
        return (x, src, dst, edge_type_2, edge_weight, node_vec)
    x, src, dst, edge_type_2, edge_weight, node_vec = _rec_inputs()

    def _L0_gnn_setup():
        import jax, jax.numpy as jnp
        import numpy as np
        NUM_RELATIONS = 2
        NUM_BASES = 30
        HIDDEN = 512
        N_NODES = 1250
        N_EDGES = 20000

        def rgcn_gate_layer(x, row, col, edge_type, basis, att, gate_w, root, bias):
            H = x.shape[1]
            w = jnp.einsum('rb,bio->rio', att, basis)
            x_j = x[col]
            msgs = []
            for r in range(NUM_RELATIONS):
                gate = jax.nn.sigmoid(x_j @ gate_w[r, :, 0])
                msgs.append(gate[:, None] * x_j @ w[r])
            msg = jnp.where((edge_type == 0)[:, None], msgs[0], msgs[1])
            agg = jax.ops.segment_sum(msg, row, num_segments=x.shape[0])
            return agg + x @ root + bias
        key = jax.random.key(seed)
        ks = jax.random.split(key, 16)
        H, R, B = (HIDDEN, NUM_RELATIONS, NUM_BASES)
        bound = 1.0 / np.sqrt(B * H)
        u = lambda k, shape: jax.random.uniform(k, shape, jnp.float32, -bound, bound)
        inp = {'x': jax.random.normal(ks[0], (N_NODES, H), jnp.float32), 'edge_index': jax.random.randint(ks[1], (2, N_EDGES), 0, N_NODES, jnp.int32), 'edge_type': jax.random.randint(ks[2], (N_EDGES,), 0, R, jnp.int32), 'basis1': u(ks[3], (B, H, H)), 'att1': u(ks[4], (R, B)), 'gate_w1': u(ks[5], (R, H, 1)), 'root1': u(ks[6], (H, H)), 'bias1': u(ks[7], (H,)), 'basis2': u(ks[8], (B, H, H)), 'att2': u(ks[9], (R, B)), 'gate_w2': u(ks[10], (R, H, 1)), 'root2': u(ks[11], (H, H)), 'bias2': u(ks[12], (H,))}
        return inp
    _L0_gnn_all = _L0_gnn_setup()
    _L0_gnn_in = {k: v for k, v in _L0_gnn_all.items() if k in ('basis1', 'att1', 'gate_w1', 'root1', 'bias1', 'basis2', 'att2', 'gate_w2', 'root2', 'bias2')}
    del _L0_gnn_all

    def _L1_gnn_setup():
        import jax, jax.numpy as jnp
        import numpy as np
        N_NODES = 6250
        N_EDGES = 50000
        DIM = 512

        def _graph_conv(x, W0, W1, b, diag, edge_vals, edge_src, edge_dst):
            n = x.shape[0]
            self_term = diag[:, None] * (x @ W0)
            msgs = edge_vals[:, None] * (x @ W1)[edge_src]
            neigh = jax.ops.segment_sum(msgs, edge_dst, num_segments=n)
            return jax.nn.relu(self_term + neigh + b)
        key = jax.random.key(seed)
        ks = jax.random.split(key, 10)
        scale = 1.0 / np.sqrt(DIM)
        return {'x': jax.random.normal(ks[0], (N_NODES, DIM), jnp.float32), 'W0_1': jax.random.normal(ks[1], (DIM, DIM), jnp.float32) * scale, 'W1_1': jax.random.normal(ks[2], (DIM, DIM), jnp.float32) * scale, 'b1': jnp.zeros((DIM,), jnp.float32), 'W0_2': jax.random.normal(ks[3], (DIM, DIM), jnp.float32) * scale, 'W1_2': jax.random.normal(ks[4], (DIM, DIM), jnp.float32) * scale, 'b2': jnp.zeros((DIM,), jnp.float32), 'diag': jax.random.uniform(ks[5], (N_NODES,), jnp.float32), 'edge_vals': jax.random.uniform(ks[6], (N_EDGES,), jnp.float32) * 0.1, 'edge_src': jax.random.randint(ks[7], (N_EDGES,), 0, N_NODES, jnp.int32), 'edge_dst': jax.random.randint(ks[8], (N_EDGES,), 0, N_NODES, jnp.int32)}
    _L1_gnn_all = _L1_gnn_setup()
    _L1_gnn_in = {k: v for k, v in _L1_gnn_all.items() if k in ('W0_1', 'W1_1', 'b1', 'W0_2', 'W1_2', 'b2')}
    del _L1_gnn_all

    def _L2_gnn_setup():
        import jax, jax.numpy as jnp
        import numpy as np
        N_NODES = 2500
        N_EDGES = 40000
        D = 512
        L = 3
        key = jax.random.key(seed)
        ks = jax.random.split(key, 6)
        x = jax.random.normal(ks[0], (N_NODES, D), dtype=jnp.float32)
        Ws_self = jax.random.normal(ks[1], (L, D, D), dtype=jnp.float32) * 0.05
        Ws_neigh = jax.random.normal(ks[2], (L, D, D), dtype=jnp.float32) * 0.05
        bs = jax.random.normal(ks[3], (L, D), dtype=jnp.float32) * 0.05
        src = jax.random.randint(ks[4], (N_EDGES,), 0, N_NODES, dtype=jnp.int64)
        dst = jax.random.randint(ks[5], (N_EDGES,), 0, N_NODES, dtype=jnp.int64)
        return {'x': x, 'Ws_self': Ws_self, 'Ws_neigh': Ws_neigh, 'bs': bs, 'src': src, 'dst': dst}
    _L2_gnn_all = _L2_gnn_setup()
    _L2_gnn_in = {k: v for k, v in _L2_gnn_all.items() if k in ('Ws_self', 'Ws_neigh', 'bs')}
    del _L2_gnn_all

    def _L3_gnn_setup():
        import jax, jax.numpy as jnp
        import numpy as np
        N_NODES = 2500
        N_EDGES = 25000
        IN_DIM = 512
        LATENT = 128
        HEADS = 4
        key = jax.random.key(seed)
        k1, k2, k3, k4 = jax.random.split(key, 4)
        x = jax.random.normal(k1, (N_NODES, IN_DIM), dtype=jnp.float32)
        edges = jax.random.randint(k2, (N_EDGES, 2), 0, N_NODES, dtype=jnp.int32)
        W = jax.random.uniform(k3, (HEADS, IN_DIM, LATENT), dtype=jnp.float32)
        a = jax.random.uniform(k4, (HEADS, 2 * LATENT), dtype=jnp.float32)
        return {'x': x, 'edges': edges, 'W': W, 'a': a}
    _L3_gnn_all = _L3_gnn_setup()
    _L3_gnn_in = {k: v for k, v in _L3_gnn_all.items() if k in ('W', 'a')}
    del _L3_gnn_all
    return {'x': x, 'src': src, 'dst': dst, 'edge_type_2': edge_type_2, 'edge_weight': edge_weight, 'node_vec': node_vec, 'L0_gnn_basis1': _L0_gnn_in['basis1'], 'L0_gnn_att1': _L0_gnn_in['att1'], 'L0_gnn_gate_w1': _L0_gnn_in['gate_w1'], 'L0_gnn_root1': _L0_gnn_in['root1'], 'L0_gnn_bias1': _L0_gnn_in['bias1'], 'L0_gnn_basis2': _L0_gnn_in['basis2'], 'L0_gnn_att2': _L0_gnn_in['att2'], 'L0_gnn_gate_w2': _L0_gnn_in['gate_w2'], 'L0_gnn_root2': _L0_gnn_in['root2'], 'L0_gnn_bias2': _L0_gnn_in['bias2'], 'L1_gnn_W0_1': _L1_gnn_in['W0_1'], 'L1_gnn_W1_1': _L1_gnn_in['W1_1'], 'L1_gnn_b1': _L1_gnn_in['b1'], 'L1_gnn_W0_2': _L1_gnn_in['W0_2'], 'L1_gnn_W1_2': _L1_gnn_in['W1_2'], 'L1_gnn_b2': _L1_gnn_in['b2'], 'L2_gnn_Ws_self': _L2_gnn_in['Ws_self'], 'L2_gnn_Ws_neigh': _L2_gnn_in['Ws_neigh'], 'L2_gnn_bs': _L2_gnn_in['bs'], 'L3_gnn_W': _L3_gnn_in['W'], 'L3_gnn_a': _L3_gnn_in['a']}

def reference(x, src, dst, edge_type_2, edge_weight, node_vec, L0_gnn_basis1, L0_gnn_att1, L0_gnn_gate_w1, L0_gnn_root1, L0_gnn_bias1, L0_gnn_basis2, L0_gnn_att2, L0_gnn_gate_w2, L0_gnn_root2, L0_gnn_bias2, L1_gnn_W0_1, L1_gnn_W1_1, L1_gnn_b1, L1_gnn_W0_2, L1_gnn_W1_2, L1_gnn_b2, L2_gnn_Ws_self, L2_gnn_Ws_neigh, L2_gnn_bs, L3_gnn_W, L3_gnn_a):
    import jax
    import jax.numpy as jnp

    def _L0_gnn_ref(x, edge_index, edge_type, basis1, att1, gate_w1, root1, bias1, basis2, att2, gate_w2, root2, bias2):
        import jax, jax.numpy as jnp
        import numpy as np
        NUM_RELATIONS = 2
        NUM_BASES = 30
        HIDDEN = 512
        N_NODES = 1250
        N_EDGES = 20000

        def rgcn_gate_layer(x, row, col, edge_type, basis, att, gate_w, root, bias):
            H = x.shape[1]
            w = jnp.einsum('rb,bio->rio', att, basis)
            x_j = x[col]
            msgs = []
            for r in range(NUM_RELATIONS):
                gate = jax.nn.sigmoid(x_j @ gate_w[r, :, 0])
                msgs.append(gate[:, None] * x_j @ w[r])
            msg = jnp.where((edge_type == 0)[:, None], msgs[0], msgs[1])
            agg = jax.ops.segment_sum(msg, row, num_segments=x.shape[0])
            return agg + x @ root + bias
        row, col = (edge_index[0], edge_index[1])
        h = jax.nn.relu(rgcn_gate_layer(x, row, col, edge_type, basis1, att1, gate_w1, root1, bias1))
        out = rgcn_gate_layer(h, row, col, edge_type, basis2, att2, gate_w2, root2, bias2)
        return out

    def _L1_gnn_ref(x, W0_1, W1_1, b1, W0_2, W1_2, b2, diag, edge_vals, edge_src, edge_dst):
        import jax, jax.numpy as jnp
        import numpy as np
        N_NODES = 6250
        N_EDGES = 50000
        DIM = 512

        def _graph_conv(x, W0, W1, b, diag, edge_vals, edge_src, edge_dst):
            n = x.shape[0]
            self_term = diag[:, None] * (x @ W0)
            msgs = edge_vals[:, None] * (x @ W1)[edge_src]
            neigh = jax.ops.segment_sum(msgs, edge_dst, num_segments=n)
            return jax.nn.relu(self_term + neigh + b)
        h = _graph_conv(x, W0_1, W1_1, b1, diag, edge_vals, edge_src, edge_dst)
        h = _graph_conv(h, W0_2, W1_2, b2, diag, edge_vals, edge_src, edge_dst)
        return (h + x) * 0.5

    def _L2_gnn_ref(x, Ws_self, Ws_neigh, bs, src, dst):
        import jax, jax.numpy as jnp
        import numpy as np
        N_NODES = 2500
        N_EDGES = 40000
        D = 512
        L = 3
        n = x.shape[0]
        deg = jax.ops.segment_sum(jnp.ones_like(dst, dtype=x.dtype), dst, num_segments=n)
        inv_deg = (1.0 / jnp.clip(deg, 1.0))[:, None]
        h = x
        n_layers = Ws_self.shape[0]
        for l in range(n_layers):
            neigh = jax.ops.segment_sum(h[src], dst, num_segments=n) * inv_deg
            h = h @ Ws_self[l] + neigh @ Ws_neigh[l] + bs[l]
            if l != n_layers - 1:
                h = jax.nn.relu(h)
        return h

    def _L3_gnn_ref(x, edges, W, a):
        import jax, jax.numpy as jnp
        import numpy as np
        N_NODES = 2500
        N_EDGES = 25000
        IN_DIM = 512
        LATENT = 128
        HEADS = 4
        num_heads, _, latent_dim = W.shape
        n_nodes = x.shape[0]
        h = jnp.einsum('hif,ni->hnf', W, x)
        src = edges[:, 0]
        dst = edges[:, 1]
        h_src = h[:, src]
        h_dst = h[:, dst]
        a_src, a_dst = (a[:, :latent_dim], a[:, latent_dim:])
        logits = jnp.einsum('hl,hel->he', a_src, h_src) + jnp.einsum('hl,hel->he', a_dst, h_dst)
        logits = jax.nn.leaky_relu(logits, negative_slope=0.2)
        lw = logits.T
        seg_max = jax.ops.segment_max(lw, src, num_segments=n_nodes)
        ex = jnp.exp(lw - seg_max[src])
        denom = jax.ops.segment_sum(ex, src, num_segments=n_nodes)
        attn = ex / denom[src]
        msg = attn[:, :, None] * jnp.transpose(h_dst, (1, 0, 2))
        agg = jax.ops.segment_sum(msg, src, num_segments=n_nodes)
        return agg.reshape(n_nodes, num_heads * latent_dim)
    edge_index = jnp.stack([src, dst])
    edge_index_t = jnp.stack([src, dst], axis=1)
    h = jnp.maximum(_layernorm(x, axis=-1), 0.0)
    x = x + _L0_gnn_ref(h, edge_index, edge_type_2, L0_gnn_basis1, L0_gnn_att1, L0_gnn_gate_w1, L0_gnn_root1, L0_gnn_bias1, L0_gnn_basis2, L0_gnn_att2, L0_gnn_gate_w2, L0_gnn_root2, L0_gnn_bias2)
    h = jnp.maximum(_layernorm(x, axis=-1), 0.0)
    x = x + _L1_gnn_ref(h, L1_gnn_W0_1, L1_gnn_W1_1, L1_gnn_b1, L1_gnn_W0_2, L1_gnn_W1_2, L1_gnn_b2, node_vec, edge_weight, src, dst)
    h = jnp.maximum(_layernorm(x, axis=-1), 0.0)
    x = x + _L2_gnn_ref(h, L2_gnn_Ws_self, L2_gnn_Ws_neigh, L2_gnn_bs, src, dst)
    h = jnp.maximum(_layernorm(x, axis=-1), 0.0)
    x = x + _L3_gnn_ref(h, edge_index_t, L3_gnn_W, L3_gnn_a)
    return x

_drawn_inputs = setup_inputs


def setup_inputs(seed=0):
    import zlib

    import numpy as np

    out = dict(_drawn_inputs(seed))
    spreads = {'L1_gnn_b1': (0.0, 2.0), 'L1_gnn_b2': (0.0, 2.0)}
    factors = {'edge_weight': 8.0,
     'node_vec': 6.218,
     'L0_gnn_basis1': 8.0,
     'L0_gnn_att1': 8.0,
     'L0_gnn_gate_w1': 8.0,
     'L0_gnn_root1': 8.0,
     'L0_gnn_bias1': 22.508,
     'L0_gnn_basis2': 8.0,
     'L0_gnn_att2': 8.0,
     'L0_gnn_gate_w2': 36.078,
     'L0_gnn_root2': 8.0,
     'L0_gnn_bias2': 22.011,
     'L1_gnn_W0_1': 4.626,
     'L1_gnn_W1_1': 4.925,
     'L1_gnn_W0_2': 4.228,
     'L1_gnn_W1_2': 4.06,
     'L2_gnn_bs': 35.272,
     'L3_gnn_a': 200.0,
     'L2_gnn_Ws_self': 7.787,
     'L2_gnn_Ws_neigh': 7.493,
     'L3_gnn_W': 8.0}
    for name, (base, spread) in spreads.items():
        noise = np.random.default_rng([zlib.crc32(name.encode()), seed]).standard_normal(out[name].shape)
        drawn = base * np.exp(spread * noise) if base else spread * noise
        out[name] = jnp.asarray(drawn.astype(out[name].dtype))
    for name, factor in factors.items():
        out[name] = (out[name] * factor).astype(out[name].dtype)
    return out
```

```python
from contextlib import ExitStack

import numpy as np

import concourse.bass as bass
from concourse import mybir

F32 = mybir.dt.float32
BF16 = mybir.dt.bfloat16
I32 = mybir.dt.int32
ALU = mybir.AluOpType
ACT = mybir.ActivationFunctionType
AX = mybir.AxisListType

NODES, H, EDGES, HEADS, LAT = 1250, 512, 20000, 4, 128
P = 125
NT = NODES // P
KT = H // 128
EC = EDGES // P
BUCKETS = NT * NT
CAP = 256
SLOTS = BUCKETS * CAP
CHUNKS = SLOTS // 128
BASES = 30
LN_EPS = 1e-5
NEG = -3.0e38
SLOPE = 0.2

RGCN0, RGCN1, CONV0, CONV1, SAGE0, SAGE1, SAGE2, GAT = range(8)
LAYERS = [RGCN0, RGCN1, CONV0, CONV1, SAGE0, SAGE1, SAGE2]


def is_rgcn(l):
    return l in (RGCN0, RGCN1)


def is_conv(l):
    return l in (CONV0, CONV1)


def is_sage(l):
    return l in (SAGE0, SAGE1, SAGE2)


def act_groups(l):
    return 3 if is_rgcn(l) else 1


def vec_groups(l):
    return 0 if l == GAT else 1


def build(nc, a, out):
    ctx = ExitStack()
    with ctx:
        def sb(name, shape, dt=F32):
            return ctx.enter_context(nc.sbuf_tensor(name, shape, dt))

        def sem(name):
            return ctx.enter_context(nc.semaphore(name))

        def scratch(name, shape, dt):
            return nc.dram_tensor(name, shape, dt, kind="Internal").ap()

        table_d = scratch("edge_table", [SLOTS, 4], F32)
        weight_d = scratch("adj_weight", [NT, P, NODES], F32)
        count_d = scratch("adj_count", [P, NT, NODES], BF16)
        typed_d = scratch("adj_typed", [P, 2, NT, NODES], BF16)
        count_rest_d = scratch("count_rest", [P, NT, NODES], BF16)
        typed_rest_d = scratch("typed_rest", [P, 2, NT, NODES], BF16)
        total_d = scratch("count_total", [P, NT, NODES], F32)
        x_d = scratch("x_resid", [3, NODES, H], F32)
        hin_d = scratch("conv_in", [NODES, H], F32)
        rows_d = scratch("gat_rows", [2, 8, NODES], F32)

        big = sb("big", [128, 12500 + NT * H])
        adj = big[:, 0:12500].bitcast(BF16).rearrange("p (r k n) -> p r k n", r=2, k=NT)
        selfs = big[:, 12500:].rearrange("p (t f) -> p t f", t=NT)
        running = big[0:P, 0:BUCKETS * EC].rearrange("p (b c) -> p b c", b=BUCKETS)
        zr = sb("zr", [128, 15360])
        parts = zr[:, :].bitcast(BF16).rearrange("p (r s k f) -> p r s k f", r=2, s=3, k=NT)
        zfull = zr[:, 0:NT * H].rearrange("p (k f) -> p k f", k=NT)
        hot = zr[0:P, 0:8000].bitcast(BF16).rearrange("p (b c) -> p b c", b=BUCKETS)
        basis_ring = zr[:, 8000:8000 + 4096].rearrange("p (n k f) -> p n k f", n=4, k=2)
        rk = zr[:, 12096:15360]
        h_all = sb("h_all", [128, NT, H])
        stage_w = h_all[:, 0:5, :].rearrange("p a b -> p (a b)")[:, 0:2500].rearrange("p (n k c) -> p n k c", n=2, k=NT)
        stage_c = h_all[:, 5:8, :].rearrange("p a b -> p (a b)")[:, 0:1250].bitcast(BF16).rearrange("p (n k c) -> p n k c", n=2, k=NT)
        wts = sb("wts", [128, 3, KT, H])
        hT = sb("hT", [128, 2, KT, P])
        bias = sb("bias", [128, 2, H])
        work = sb("work", [128, 8, H])
        zt = work[:, 0:2]
        xin = work[:, 2:4]
        hin = work[:, 4:6]
        ht_tmp = work[:, 6:8]
        onehots = work[:, :, :].rearrange("p a b -> p (a b)").bitcast(BF16)[:, 0:2 * 6 * 128].rearrange("p (n v c) -> p n v c", n=2, v=6)
        edges = sb("edges", [128, 2240])
        rec = edges[0:P, 0:640].rearrange("p (c f) -> p c f", f=4)
        slot = edges[0:P, 640:800].bitcast(I32)
        table = edges[:, 800:1600].rearrange("p (j f) -> p j f", f=4)
        iota4 = edges[:, 0:256].bitcast(BF16).rearrange("p (c j) -> p c j", j=4)
        node_bf = edges[:, 1600:1800].bitcast(BF16).rearrange("p (v j) -> p v j", v=2)
        coef_bf = edges[:, 1800:2200].bitcast(BF16).rearrange("p (v j) -> p v j", v=4)
        basis2_ring = edges[:, 0:2048].rearrange("p (n k f) -> p n k f", n=2, k=2)
        raw_in = edges[0:P, 0:640]
        raw_node = edges[0:P, 640:960].rearrange("p (v c) -> p v c", v=2)
        raw_type = edges[0:P, 960:1280].rearrange("p (v c) -> p v c", v=2)
        raw_w = edges[0:P, 1280:1760].rearrange("p (s c) -> p s c", s=3)
        rel_node = edges[0:P, 1760:2080].rearrange("p (v c) -> p v c", v=2)
        tile_base = edges[0:P, 2080:2080 + NT]
        rest_row = work[:, :, :].rearrange("p a b -> p (a b)")[0:P, 1024:1024 + NODES].bitcast(BF16).rearrange("p (v c) -> p v c", v=2)
        ident = sb("ident", [128, 128])
        hT_flat = hT[:, :, :, :].rearrange("p a k c -> p (a k c)")
        diag = hT_flat[:, 0:512].rearrange("p (n c) -> p n c", n=4)
        tri = hT_flat[:, 512:640]
        ones_f = hT_flat[:, 640:768]
        rest_slab = hT_flat[0:P, 0:625].bitcast(BF16).rearrange("p (k c) -> p k c", k=NT)
        iota_c = sb("iota_c", [128, 128], BF16)
        ones_bf = sb("ones_bf", [128, EC], BF16)
        att = sb("att", [128, 2, 2 * BASES])
        gate_w = sb("gate_w", [128, 2, KT, 2])
        gates = sb("gates", [128, 2, 2])
        node_scale = sb("node_scale", [128, NT])
        inv_deg = sb("inv_deg", [128, NT])
        stats = sb("stats", [128, 6])
        mv = sb("mv", [128, 4])
        eps = sb("eps", [128, 1])
        fullest = sb("fullest", [128, 1])
        overflow = sb("overflow", [128, 1], I32)

        ps = ctx.enter_context(nc.psum_tensor("ps", [128, 8, 512], F32))

        const_ready = sem("const_ready")
        edge_in = sem("edge_in")
        dve_step = sem("dve_step")
        act_step = sem("act_step")
        pool_step = sem("pool_step")
        totals_ready = sem("totals_ready")
        prefix_ready = sem("prefix_ready")
        slots_ready = sem("slots_ready")
        table_clear = sem("table_clear")
        scattered = sem("scattered")
        overflow_ready = sem("overflow_ready")
        raw_ready = sem("raw_ready")
        raw_step = sem("raw_step")
        chunk_hot = sem("chunk_hot")
        chunk_used = sem("chunk_used")
        row_stored = sem("row_stored")
        rest_in = sem("rest_in")
        rest_used = sem("rest_used")
        rest_out = sem("rest_out")
        rest_degree = sem("rest_degree")
        total_in = sem("total_in")
        table_in = sem("table_in")
        att_in = sem("att_in")
        basis_in = [sem(f"basis_in{n}") for n in range(4)]
        basis_used = sem("basis_used")
        basis2_in = [sem(f"basis2_in{n}") for n in range(2)]
        basis2_used = sem("basis2_used")
        diag_ready = sem("diag_ready")
        combined_out = sem("combined_out")
        first_x_in = sem("first_x_in")
        first_var = sem("first_var")
        first_std = sem("first_std")
        x_in = [sem(f"x_in{n}") for n in range(2)]
        x_ready = sem("x_ready")
        var_ready = sem("var_ready")
        std_ready = sem("std_ready")
        hin_in = [sem(f"hin_in{n}") for n in range(2)]
        weights_in = sem("weights_in")
        w2_ready = sem("w2_ready")
        node_in = sem("node_in")
        h_ready = sem("h_ready")
        transposed = sem("transposed")
        hT_ready = sem("hT_ready")
        zact_mm = sem("zact_mm")
        zact_out = sem("zact_out")
        zvec_mm = sem("zvec_mm")
        zvec_out = sem("zvec_out")
        split_done = sem("split_done")
        agg_mm = sem("agg_mm")
        agg_out = sem("agg_out")
        x_stored = [sem(f"x_stored{n}") for n in range(2)]
        hin_stored = sem("hin_stored")
        hot_ready = sem("hot_ready")
        hot_used = sem("hot_used")
        pair_act = sem("pair_act")
        pair_vec = sem("pair_vec")
        stage_out = [sem(f"stage_out{n}") for n in range(2)]
        typed_stored = sem("typed_stored")
        count_in = sem("count_in")
        slab_in = [sem(f"slab_in{n}") for n in range(4)]
        deg_mm = sem("deg_mm")
        deg_out = sem("deg_out")
        gat_in = sem("gat_in")
        score_ready = sem("score_ready")
        score_tr = sem("score_tr")
        score_row = sem("score_row")
        rows_stored = sem("rows_stored")
        adrow_in = sem("adrow_in")
        max_ready = sem("max_ready")
        headrow_in = [sem(f"headrow_in{n}") for n in range(2)]
        typed_in = sem("typed_in")
        x3_in = sem("x3_in")
        pos_ready = sem("pos_ready")
        neg_ready = sem("neg_ready")
        below = sem("below")
        expd = sem("expd")
        attn = sem("attn")
        attn_used = sem("attn_used")
        head_mm = sem("head_mm")
        head_out = sem("head_out")
        stored = sem("stored")

        gat_typed = sem("gat_typed")

        def pair_hot(m):
            home = work if m % 4 < 2 else wts[:, 0:2]
            flat = home.rearrange("p r k f -> p (r k f)") if m % 4 >= 2 else home[:, :, :].rearrange("p a b -> p (a b)")
            return flat.bitcast(BF16)[:, 3072 * (m % 2):3072 * (m % 2 + 1)].rearrange("p (v c j) -> p v c j", v=6, c=128)

        def slab(n):
            return big[0:P, 6250 + 1250 * (n % 4):6250 + 1250 * (n % 4) + 1250]

        hh = zr[:, 0:NT * HEADS * (LAT + 1)].rearrange("p (t h f) -> p t h f", t=NT, h=HEADS)
        z0 = NT * HEADS * (LAT + 1)
        head_rows = zr[:, z0:z0 + 5000].rearrange("p (n v c) -> p n v c", n=2, v=2)
        ad_rows = zr[:, z0:z0 + 5000].rearrange("p (h c) -> p h c", h=HEADS)
        pos_t = h_all[:, :, :].rearrange("p a b -> p (a b)")[:, 0:3750].rearrange("p (n c) -> p n c", n=3)
        total_row = h_all[:, :, :].rearrange("p a b -> p (a b)")[0:P, 3750:5000]
        neg_t = zr[:, z0 + 5000:z0 + 7500].rearrange("p (n c) -> p n c", n=2)
        neg_vec = work[:, :, :].rearrange("p a b -> p (a b)")[0:P, 4096 - NODES:4096]
        attn_t = zr[:, z0 + 7500:z0 + 10000].rearrange("p (n c) -> p n c", n=2)
        type1_in = zr[0:P, 7680:7680 + 6250].bitcast(BF16).rearrange("p (k n) -> p k n", k=NT)
        a_both = work[:, 0:2, :]
        score = work[:, 2, 0:8 * NT].rearrange("p (t v) -> p t v", v=8)
        top = work[:, 3, 0:4 * NT].rearrange("p (t v) -> p t v", v=4)
        bucket = rk[0:P, 1600:1760]
        totals = rk[0:P, 1760:1860]
        before = rk[0:P, 1860:1960]
        rank = rk[0:P, 1960:2120]
        high = rk[0:P, 2120:2280]
        first_stats = rk[0:P, 2280:2280 + 6 * NT].rearrange("p (t v) -> p t v", v=6)
        first_mv = rk[0:P, 2340:2340 + 4 * NT].rearrange("p (t v) -> p t v", v=4)
        score2 = work[:, 5, 0:8 * NT].rearrange("p (t v) -> p t v", v=8)
        minus_dst = work[:, 4, 192:192 + 4 * NT].rearrange("p (t v) -> p t v", v=4)
        minus_slope_dst = work[:, 4, 128:128 + 4 * NT].rearrange("p (t v) -> p t v", v=4)
        rden = work[:, 4, 64:64 + NT]
        score_rows = wts[0:8 * NT, 0, 0, 0:P]

        block = ctx.enter_context(nc.Block())

        def overflowed(eng):
            eng.wait_ge(overflow_ready, 1)
            return eng.value_load(overflow[0:1, 0:1], min_val=0, max_val=1)

        def rest_tiles_before(l):
            return NT * sum(not is_conv(m) for m in range(l))

        def rest_before(l):
            n = NT * sum(2 if is_rgcn(m) else 1 if is_sage(m) else 0 for m in range(l))
            return n + (NT if l > SAGE0 else 0)

        def rows(ap2d, t):
            return ap2d[t * P:(t + 1) * P, :]

        def z_before(l, kind):
            return NT * sum(kind(m) for m in range(l))

        def agg_before(l):
            return NT * l

        def splits_before(l):
            return NT * sum(2 if is_rgcn(m) else 1 if is_sage(m) else 0 for m in range(l))

        def loads_before(l):
            return sum(4 if is_rgcn(m) or m == GAT else 3 for m in range(l))

        def wait_tiles(eng, n):
            if n <= NT * GAT:
                eng.wait_ge(zvec_mm, n)
            else:
                eng.wait_ge(zact_mm, z_before(GAT, act_groups) + n - NT * GAT)

        FIRST_STD = 46
        NBAS = 2 * BASES

        @block.sync
        def _(sp):
            sp.dma_start(rk[0:P, 0:160].bitcast(I32), a["src"].rearrange("(p c) -> p c", p=P)).then_inc(edge_in, 16)
            sp.dma_start(rk[0:P, 160:320].bitcast(I32), a["dst"].rearrange("(p c) -> p c", p=P)).then_inc(edge_in, 16)
            sp.dma_start(rk[0:P, 320:480].bitcast(I32), a["edge_type_2"].rearrange("(p c) -> p c", p=P)).then_inc(edge_in, 16)
            sp.dma_start(rk[0:P, 480:640], a["edge_weight"].rearrange("(p c) -> p c", p=P)).then_inc(edge_in, 16)
            for n in range(NBAS):
                kh, b = divmod(n, BASES)
                if n == 8:
                    sp.dma_start(h_all[0:P], a["x"].rearrange("(t p) f -> p t f", p=P)).then_inc(first_x_in, 16)
                if n >= 4:
                    sp.wait_ge(basis_used, n - 3)
                sp.dma_start(basis_ring[:, n % 4],
                             a["L0_gnn_basis1"][b].rearrange("(k p) f -> p k f", p=128)[:, 2 * kh:2 * kh + 2, :]
                             ).then_inc(basis_in[n % 4], 16)
            sp.wait_ge(scattered, 16 * EC)
            general = overflowed(sp)
            with sp.If(general == 0):
                sp.dma_start(table, table_d.rearrange("(p j) f -> p j f", p=128)).then_inc(table_in, 16)
                for qd in range(NT):
                    sp.wait_ge(pair_act, 5 * (qd + 1))
                    sp.dma_start(weight_d[qd], stage_w[0:P, qd % 2].rearrange("p k c -> p (k c)")).then_inc(stage_out[qd % 2], 16)
                    sp.dma_start(count_d[:, qd, :], stage_c[0:P, qd % 2].rearrange("p k c -> p (k c)")).then_inc(stage_out[qd % 2], 16)
                for n in range(2):
                    sp.wait_ge(stage_out[n], 16 * NT)
            with sp.Else():
                for n, name in enumerate(("src", "dst", "edge_type_2")):
                    sp.dma_start(raw_in[:, n * EC:(n + 1) * EC].bitcast(I32), a[name].rearrange("(p c) -> p c", p=P)).then_inc(raw_ready, 16)
                sp.dma_start(raw_in[:, 3 * EC:], a["edge_weight"].rearrange("(p c) -> p c", p=P)).then_inc(raw_ready, 16)
                with sp.Fori(0, NT) as qd:
                    sp.wait_ge(pair_vec, 5 * qd + 6)
                    sp.dma_start(weight_d[bass.ds(qd, 1)].rearrange("o p n -> p (o n)"), stage_w[0:P, 0].rearrange("p k c -> p (k c)")).then_inc(row_stored, 16)
                    sp.dma_start(total_d[:, bass.ds(qd, 1), :].rearrange("p o n -> p (o n)"), stage_w[0:P, 1].rearrange("p k c -> p (k c)")).then_inc(row_stored, 16)
                    sp.dma_start(count_d[:, bass.ds(qd, 1), :].rearrange("p o n -> p (o n)"), stage_c[0:P, 0].rearrange("p k c -> p (k c)")).then_inc(row_stored, 16)
                    sp.dma_start(count_rest_d[:, bass.ds(qd, 1), :].rearrange("p o n -> p (o n)"), stage_c[0:P, 1].rearrange("p k c -> p (k c)")).then_inc(row_stored, 16)
                    for r in range(2):
                        sp.dma_start(typed_rest_d[:, r, bass.ds(qd, 1), :].rearrange("p o n -> p (o n)"), rest_row[:, r, :]).then_inc(row_stored, 16)
                sp.wait_ge(row_stored, 96 * NT)

            def load_rests(l, src):
                wait_tiles(sp, NT * (l + 1))
                rels = 2 if is_rgcn(l) else 1
                for n in range(NT * rels if l != SAGE0 else 2 * NT):
                    t, r = divmod(n % NT if l == SAGE0 else n, rels)
                    if rest_before(l) + n:
                        sp.wait_ge(rest_used, rest_before(l) + n)
                    sp.dma_start(rest_slab, src(r, t)).then_inc(rest_in, 16)

            def typed_rest(r, t):
                return typed_rest_d[:, r, :, t * P:(t + 1) * P]

            def count_rest(r, t):
                return count_rest_d[:, t, :].rearrange("p (k c) -> p k c", k=NT)

            sp.wait_ge(pair_vec, NT * NT // 2)
            sp.dma_start(typed_d, adj[0:P]).then_inc(typed_stored, 16)
            with sp.If(general != 0):
                load_rests(RGCN0, typed_rest)
            for n in range(2 * BASES):
                b, kh = divmod(n, 2)
                if n >= 2:
                    sp.wait_ge(basis2_used, n - 1)
                sp.dma_start(basis2_ring[:, n % 2],
                             a["L0_gnn_basis2"][b].rearrange("(k p) f -> p k f", p=128)[:, 2 * kh:2 * kh + 2, :]
                             ).then_inc(basis2_in[n % 2], 16)
            with sp.If(general != 0):
                load_rests(RGCN1, typed_rest)
            for l in (CONV0, CONV1):
                for t in range(NT):
                    n = (l - CONV0) * NT + t
                    if n == 0:
                        sp.wait_ge(agg_mm, agg_before(CONV0))
                        sp.wait_ge(typed_stored, 16)
                        sp.dma_start(adj[0:P, 0], count_d).then_inc(count_in, 16)
                    if n >= 4:
                        sp.wait_ge(agg_mm, agg_before(CONV0) + n - 3)
                    sp.dma_start(slab(n), weight_d[t]).then_inc(slab_in[n % 4], 16)
            sp.dma_start(type1_in, typed_d[:, 1]).then_inc(typed_in, 16)
            sp.wait_ge(agg_mm, agg_before(SAGE0))
            sp.dma_start(adj[0:P, 1], typed_d[:, 0]).then_inc(typed_in, 16)
            with sp.If(general != 0):
                for l in (SAGE0, SAGE1, SAGE2):
                    load_rests(l, count_rest)
            sp.wait_ge(score_row, 1)
            for t in range(NT):
                sp.dma_start(rows_d[0, :, t * P:(t + 1) * P], score_rows[8 * t:8 * t + 8, :]).then_inc(rows_stored, 16)
            sp.wait_ge(rows_stored, 16 * NT)
            for h in range(HEADS):
                sp.dma_start(ad_rows[:, h, :], rows_d[0, h].partition_broadcast(128)).then_inc(adrow_in, 16)
            sp.wait_ge(score_row, 2)
            for t in range(NT):
                sp.dma_start(rows_d[1, :, t * P:(t + 1) * P], score_rows[8 * t:8 * t + 8, :]).then_inc(rows_stored, 16)
            sp.wait_ge(rows_stored, 32 * NT)

            def load_head_rows(h):
                if h >= 2:
                    sp.wait_ge(expd, NT * (h - 1))
                for v in range(2):
                    sp.dma_start(head_rows[:, h % 2, v, :], rows_d[1, 4 * v + h].partition_broadcast(128)).then_inc(headrow_in[h % 2], 16)

            load_head_rows(0)
            load_head_rows(1)
            with sp.If(general != 0):
                for i in range(HEADS * NT):
                    if i >= 1:
                        sp.wait_ge(attn, i)
                    sp.dma_start(total_row, total_d[:, i % NT, :]).then_inc(total_in, 16)
                    if i == NT or i == 2 * NT:
                        load_head_rows(i // NT + 1)
            with sp.Else():
                load_head_rows(2)
                load_head_rows(3)
            sp.wait_ge(head_out, HEADS)
            sp.dma_start(out.rearrange("(t p) f -> p t f", p=P), selfs[0:P]).then_inc(stored, 16)
            sp.wait_ge(stored, 16)


        @block.gpsimd
        def _(pool):
            pool.dma_start(att[:, 0, :], a["L0_gnn_att1"].rearrange("r b -> (r b)").partition_broadcast(128)).then_inc(att_in, 16)
            pool.dma_start(att[:, 1, :], a["L0_gnn_att2"].rearrange("r b -> (r b)").partition_broadcast(128)).then_inc(att_in, 16)
            pool.memset(ident[:, :], 0.0).then_inc(pool_step, 1)
            pool.memset(tri[:, :], 1.0).then_inc(pool_step, 1)
            pool.memset(ones_bf[:, :], 1.0).then_inc(const_ready, 1)
            pool.memset(ones_f, 1.0).then_inc(const_ready, 1)
            pool.memset(eps[:, :], LN_EPS).then_inc(const_ready, 1)
            pool.iota(iota_c[:, :], [[1, 128]], base=0, channel_multiplier=0,
                      allow_small_or_imprecise_dtypes=True).then_inc(const_ready, 1)
            pool.memset(table, -1.0).then_inc(pool_step, 1)
            pool.wait_ge(pool_step, 3)
            pool.affine_select(out=ident[:, :], in_=ident[:, :], compare_op=ALU.not_equal, fill=1.0,
                               base=0, pattern=[[-1, 128]], channel_multiplier=1).then_inc(const_ready, 1)
            pool.affine_select(out=tri[:, :], in_=tri[:, :], compare_op=ALU.is_gt, fill=0.0,
                               base=0, pattern=[[1, 128]], channel_multiplier=-1).then_inc(const_ready, 1)
            pool.dma_start(table_d.rearrange("(p j) f -> p j f", p=128), table).then_inc(table_clear, 16)

            def load_layer(l):
                if is_rgcn(l):
                    s = str(l + 1)
                    pool.dma_start(wts[:, 2], a["L0_gnn_root" + s].rearrange("(k p) f -> p k f", p=128)).then_inc(weights_in, 16)
                    pool.dma_start(bias[:, l % 2], a["L0_gnn_bias" + s].partition_broadcast(128)).then_inc(weights_in, 16)
                    for r in range(2):
                        with nc.allow_non_contiguous_dma(reason="512 gate weights"):
                            pool.dma_start(gate_w[:, l % 2, :, r], a["L0_gnn_gate_w" + s][r].rearrange("(k p) o -> p (k o)", p=128)).then_inc(weights_in, 16)
                elif is_conv(l):
                    s = str(l - CONV0 + 1)
                    pool.dma_start(wts[:, 0], a["L1_gnn_W1_" + s].rearrange("(k p) f -> p k f", p=128)).then_inc(weights_in, 16)
                    pool.dma_start(wts[:, 2], a["L1_gnn_W0_" + s].rearrange("(k p) f -> p k f", p=128)).then_inc(weights_in, 16)
                    pool.dma_start(bias[:, l % 2], a["L1_gnn_b" + s].partition_broadcast(128)).then_inc(weights_in, 16)
                elif is_sage(l):
                    pool.dma_start(wts[:, 0], a["L2_gnn_Ws_neigh"][l - SAGE0].rearrange("(k p) f -> p k f", p=128)).then_inc(weights_in, 16)
                    pool.dma_start(wts[:, 2], a["L2_gnn_Ws_self"][l - SAGE0].rearrange("(k p) f -> p k f", p=128)).then_inc(weights_in, 16)
                    pool.dma_start(bias[:, l % 2], a["L2_gnn_bs"][l - SAGE0].partition_broadcast(128)).then_inc(weights_in, 16)
                else:
                    for hd in range(HEADS):
                        pool.dma_start(wts[:, 0, :, hd * LAT:(hd + 1) * LAT],
                                       a["L3_gnn_W"][hd].rearrange("(k p) f -> p k f", p=128)).then_inc(weights_in, 16)

            def load_x(q, src):
                if q >= 2:
                    pool.wait_ge(x_ready, q - 1)
                    pool.wait_ge(x_stored[q % 2], 16 * ((q - 2) // 2 + 1))
                pool.dma_start(xin[0:P, q % 2], src).then_inc(x_in[q % 2], 16)

            load_layer(RGCN0)
            with nc.allow_non_contiguous_dma(reason="one scale per node"):
                pool.dma_start(node_scale[0:P, :], a["node_vec"].rearrange("(t p) -> p t", p=P)).then_inc(node_in, 16)
            pool.wait_ge(table_clear, 16)
            pool.wait_ge(slots_ready, 1)
            for c in range(EC):
                pool.indirect_dma_start(table_d, bass.IndirectOffsetOnAxis(slot[:, c:c + 1], 0), rec[:, c, :], None,
                                        bounds_check=SLOTS - 1, oob_is_err=False).then_inc(scattered, 16)
            for l in LAYERS:
                wait_tiles(pool, NT * (l + 1))
                load_layer(l + 1)
                if l in (RGCN1, CONV1, SAGE2):
                    blk = (RGCN1, CONV1, SAGE2).index(l)
                    if blk:
                        for n in range(2):
                            pool.wait_ge(x_stored[n], 16 * 5 * blk)

                    def load(t):
                        load_x(NT * blk + t, rows(a["x"] if blk == 0 else x_d[blk - 1], t))
                        if l == CONV1:
                            pool.dma_start(hin[0:P, t % 2], rows(hin_d, t)).then_inc(hin_in[t % 2], 16)

                    load(0)
                    load(1)
                    for t in range(NT):
                        q = NT * blk + t
                        pool.wait_ge(x_ready, q + 1)
                        pool.dma_start(rows(x_d[blk], t), xin[0:P, q % 2]).then_inc(x_stored[q % 2], 16)
                        if l == RGCN1:
                            pool.wait_ge(h_ready, NT * (l + 1) + t + 1)
                            pool.dma_start(rows(hin_d, t), h_all[0:P, t]).then_inc(hin_stored, 16)
                        if t + 2 < NT:
                            load(t + 2)
                    if l == RGCN1:
                        pool.wait_ge(hin_stored, 16 * NT)
            pool.wait_ge(x_stored[0], 16 * 15)
            pool.wait_ge(x_stored[1], 16 * 15)
            pool.dma_start(selfs[0:P], x_d[2].rearrange("(t p) f -> p t f", p=P)).then_inc(x3_in, 16)
            pool.wait_ge(agg_mm, agg_before(GAT))
            pool.memset(hh[:, :, :, LAT:LAT + 1], 1.0).then_inc(gat_in, 1)
            pool.memset(score2[:, :, :], 0.0).then_inc(gat_in, 1)
            pool.wait_ge(x_ready, 3 * NT)
            for v in range(2):
                pool.dma_start(a_both[:, v].rearrange("p (h f) -> p h f", h=HEADS),
                               a["L3_gnn_a"][:, (1 - v) * LAT:(2 - v) * LAT].partition_broadcast(128)).then_inc(weights_in, 16)

        @block.tensor
        def _(pe):
            pe.wait_ge(const_ready, 6)

            def prefix_product():
                pe.wait_ge(totals_ready, 1)
                pe.matmul(ps[0:P, 4, 0:BUCKETS], lhsT=tri[0:P, 0:P], rhs=totals, start=True, stop=True)
                pe.matmul(ps[:, 4, 128:128 + BUCKETS], lhsT=ones_f[0:P, :], rhs=totals, start=True, stop=True).then_inc(prefix_ready, 1)

            for n in range(NBAS):
                kh, b = divmod(n, BASES)
                if n == BASES:
                    pe.wait_ge(combined_out, 1)
                pe.wait_ge(basis_in[n % 4], 16 * (n // 4 + 1))
                pe.wait_ge(diag_ready, n + 1)
                for r in range(2):
                    for k in range(2):
                        last = pe.matmul(ps[:, 2 * r + k, :], lhsT=diag[:, 2 * (n % 2) + r, :], rhs=basis_ring[:, n % 4, k, :],
                                         start=(b == 0), stop=(b == BASES - 1))
                last.then_inc(basis_used, 1)
                if n == 14:
                    prefix_product()

            def transpose_tile(l, t):
                g = NT * l + t
                pe.wait_ge(h_ready, g + 1)
                if g >= 2:
                    pe.wait_ge(hT_ready, g - 1)
                for k in range(KT):
                    last = pe.transpose(ps[:, g % 2, k * P:(k + 1) * P], h_all[0:P, t, k * 128:(k + 1) * 128], ident[0:P, 0:P])
                last.then_inc(transposed, 1)

            def product(bank, l, t, w):
                g = NT * l + t
                for k in range(KT):
                    last = pe.matmul(bank, lhsT=hT[:, g % 2, k, :], rhs=w(k), start=(k == 0), stop=(k == KT - 1))
                return last

            def act_bank(q):
                if q >= 2:
                    pe.wait_ge(zact_out, q - 1)
                return ps[0:P, 2 + q % 2, :]

            def vec_bank(q):
                if q >= 2:
                    pe.wait_ge(zvec_out, q - 1)
                return ps[0:P, 4 + q % 2, :]

            def weight_products(l):
                pe.wait_ge(weights_in, 16 * loads_before(l + 1))
                if l == RGCN0:
                    pe.wait_ge(combined_out, 2)
                if l == RGCN1:
                    pe.wait_ge(w2_ready, 1)
                transpose_tile(l, 0)
                for t in range(NT):
                    if t + 1 < NT:
                        transpose_tile(l, t + 1)
                    pe.wait_ge(hT_ready, NT * l + t + 1)
                    qa = z_before(l, act_groups) + act_groups(l) * t
                    if is_rgcn(l):
                        product(act_bank(qa)[:, 0:2], l, t, lambda k: gate_w[:, l % 2, k, :]).then_inc(zact_mm, 1)
                        for r in range(2):
                            product(act_bank(qa + 1 + r), l, t, lambda k: wts[:, r, k, :]).then_inc(zact_mm, 1)
                    else:
                        last = product(act_bank(qa), l, t, lambda k: wts[:, 0, k, :])
                        last.then_inc(zact_mm, 1)
                    if l != GAT:
                        qv = z_before(l, vec_groups) + t
                        last = product(vec_bank(qv), l, t, lambda k: wts[:, 2, k, :])
                        last.then_inc(zvec_mm, 1)

            def aggregate(l):
                if is_rgcn(l) or is_sage(l):
                    pe.wait_ge(split_done, splits_before(l + 1))
                else:
                    pe.wait_ge(zact_out, z_before(l + 1, act_groups))
                if l == SAGE0:
                    pe.wait_ge(deg_out, 1)
                if not is_conv(l):
                    with pe.If(general != 0):
                        rels = 2 if is_rgcn(l) else 1
                        if l:
                            pe.wait_ge(agg_out, agg_before(l))
                        first = rest_before(l) + (NT if l == SAGE0 else 0)
                        for t in range(NT):
                            if rest_tiles_before(l) + t:
                                pe.wait_ge(rest_out, rest_tiles_before(l) + t)
                            for r in range(rels):
                                pe.wait_ge(rest_in, 16 * (first + t * rels + r + 1))
                                for k in range(NT):
                                    for s in range(3):
                                        last = pe.matmul(ps[0:P, 6, :], lhsT=rest_slab[:, k, :], rhs=parts[0:P, r, s, k, :],
                                                         start=(r == 0 and k == 0 and s == 0),
                                                         stop=(r == rels - 1 and k == NT - 1 and s == 2))
                                last.then_inc(rest_used, 1)
                        pe.wait_ge(rest_out, rest_tiles_before(l) + NT)
                for t in range(NT):
                    g = NT * l + t
                    if g >= 2:
                        pe.wait_ge(agg_out, g - 1)
                    bank = ps[0:P, 6 + g % 2, :]
                    if is_conv(l):
                        n = (l - CONV0) * NT + t
                        pe.wait_ge(slab_in[n % 4], 16 * (n // 4 + 1))
                        for k in range(NT):
                            last = pe.matmul(bank, lhsT=slab(n)[:, k * P:(k + 1) * P], rhs=zfull[0:P, k, :],
                                             start=(k == 0), stop=(k == NT - 1))
                    else:
                        rels = 2 if is_rgcn(l) else 1
                        for r in range(rels):
                            for k in range(NT):
                                lhsT = adj[0:P, r, k, t * P:(t + 1) * P] if is_rgcn(l) else adj[0:P, 0, t, k * P:(k + 1) * P]
                                for s in range(3):
                                    last = pe.matmul(bank, lhsT=lhsT, rhs=parts[0:P, r, s, k, :],
                                                     start=(r == 0 and k == 0 and s == 0),
                                                     stop=(r == rels - 1 and k == NT - 1 and s == 2))
                    last.then_inc(agg_mm, 1)

            weight_products(RGCN0)

            pe.wait_ge(zact_out, z_before(RGCN1, act_groups))
            pe.wait_ge(zvec_out, z_before(RGCN1, vec_groups))
            general = overflowed(pe)
            with pe.If(general == 0):
                for m in range(BUCKETS // 2):
                    pe.wait_ge(hot_ready, m + 1)
                    if m >= 4:
                        pe.wait_ge(pair_act, m - 3)
                        pe.wait_ge(pair_vec, m - 3)
                    hots = pair_hot(m)
                    for b in range(2):
                        for v, (left, right) in enumerate(((1, (0,)), (5, (0,)), (0, (1,)), (0, (2, 3, 4)))):
                            for j in range(2):
                                for i, rr in enumerate(right):
                                    last = pe.matmul(ps[:, 2 * (m % 4) + b, v * P:(v + 1) * P], lhsT=hots[:, left, :, 2 * b + j],
                                                     rhs=hots[:, rr, 0:P, 2 * b + j], start=(j == 0 and i == 0),
                                                     stop=(j == 1 and i == len(right) - 1))
                    last.then_inc(hot_used, 1)
                pe.wait_ge(pair_act, BUCKETS // 2)
                pe.wait_ge(pair_vec, BUCKETS // 2)
            with pe.Else():
                with pe.Fori(0, NT) as qd:
                    with pe.Fori(0, NT // 2) as qp:
                        pe.wait_ge(pair_vec, 5 * qd + qp + 1)
                        for bb in range(2):
                            def chunk(c, first, last_one):
                                pe.wait_ge(chunk_hot, (10 * qd + 2 * qp + bb) * EC + c + 2)
                                for v, (left, right) in enumerate((((1, 0), (0,)), ((0, 5), (0,)), ((0, 0), (1,)), ((0, 0), (2, 3, 4)))):
                                    for rr in right:
                                        last = pe.matmul(ps[:, bb, v * P:(v + 1) * P], lhsT=onehots[0:P, left[0], left[1], :],
                                                         rhs=onehots[0:P, 0, rr, 0:P], start=first and v == 0,
                                                         stop=last_one, skip_group_check=True)
                                last.then_inc(chunk_used, 1)

                            chunk(0, True, False)
                            with pe.Fori(1, EC - 1) as c:
                                chunk(c, False, False)
                            chunk(EC - 1, False, True)
                pe.wait_ge(pair_vec, BUCKETS // 2 + 1)

            aggregate(RGCN0)
            for l in LAYERS[1:]:
                weight_products(l)
                if l == SAGE0:
                    pe.wait_ge(count_in, 16)
                    pe.wait_ge(agg_out, agg_before(SAGE0))
                    for t in range(NT):
                        for k in range(NT):
                            last = pe.matmul(ps[0:P, 6, t:t + 1], lhsT=adj[0:P, 0, t, k * P:(k + 1) * P], rhs=ones_bf[0:P, 0:1],
                                             start=(k == 0), stop=(k == NT - 1))
                    last.then_inc(deg_mm, 1)
                    with pe.If(general != 0):
                        for t in range(NT):
                            pe.wait_ge(rest_in, 16 * (rest_before(l) + t + 1))
                            for k in range(NT):
                                last = pe.matmul(ps[0:P, 7, t:t + 1], lhsT=rest_slab[:, k, :], rhs=ones_bf[0:P, 0:1],
                                                 start=(k == 0), stop=(k == NT - 1))
                            last.then_inc(rest_used, 1)
                aggregate(l)
            weight_products(GAT)
            for n in range(2):
                pe.wait_ge(score_ready, NT if n == 0 else NT + 1)
                if n == 0:
                    pe.wait_ge(agg_out, agg_before(GAT))
                pe.transpose(ps[0:8 * NT, 6, 0:P], (score if n == 0 else score2)[0:P].rearrange("p t v -> p (t v)"),
                             ident[0:P, 0:P]).then_inc(score_tr, 1)
            pe.wait_ge(zact_out, z_before(GAT + 1, act_groups))
            pe.wait_ge(score_row, 2)
            pe.wait_ge(gat_in, 2)
            for h in range(HEADS):
                for k in range(NT):
                    pe.wait_ge(attn, h * NT + k + 1)
                    if k == 0 and h >= 2:
                        pe.wait_ge(head_out, h - 1)
                    for t in range(NT):
                        last = pe.matmul(ps[0:P, 4 * (h % 2) + t // 3, (t % 3) * (LAT + 1):(t % 3 + 1) * (LAT + 1)],
                                         lhsT=attn_t[0:P, (h * NT + k) % 2, t * P:(t + 1) * P], rhs=hh[0:P, k, h, :],
                                         start=(k == 0 and t % 3 == 0), stop=(k == NT - 1), skip_group_check=True)
                    last.then_inc(attn_used, 1)

        @block.scalar
        def _(act):
            act.wait_ge(const_ready, 6)
            act.wait_ge(att_in, 32)

            def copy_half(kh):
                act.wait_ge(basis_used, BASES * (kh + 1))
                for r in range(2):
                    last = act.activation(wts[:, r, 2 * kh:2 * kh + 2, :], ps[:, 2 * r:2 * r + 2, :], ACT.Copy)
                last.then_inc(combined_out, 1)

            def std(q):
                act.wait_ge(var_ready, q + 1)
                act.activation(mv[0:P, 2:3], mv[0:P, 1:2], ACT.Sqrt, bias=eps[0:P, :]).then_inc(std_ready, 1)

            for n in range(NBAS):
                b = n % BASES
                if n >= 2:
                    act.wait_ge(basis_used, n - 1)
                if n == BASES:
                    copy_half(0)
                if n == FIRST_STD:
                    act.wait_ge(first_var, 1)
                    act.activation(first_mv[:, :, 2], first_mv[:, :, 1], ACT.Sqrt, bias=eps[0:P, :]).then_inc(first_std, 1)
                for r in range(2):
                    last = act.activation(diag[:, 2 * (n % 2) + r, :], ident[:, :], ACT.Copy,
                                          scale=att[:, 0, r * BASES + b:r * BASES + b + 1])
                last.then_inc(diag_ready, 1)
            copy_half(1)

            def copy_hT(l, t):
                g = NT * l + t
                act.wait_ge(transposed, g + 1)
                if g >= 2:
                    wait_tiles(act, g - 1)
                act.activation(hT[:, g % 2].rearrange("p k c -> p (k c)"), ps[:, g % 2, 0:KT * P], ACT.Copy).then_inc(hT_ready, 1)

            def empty_groups(l):
                s = splits_before(l)
                copy_hT(l, 0)
                for t in range(NT):
                    if t + 1 < NT:
                        copy_hT(l, t + 1)
                    q = z_before(l, act_groups) + act_groups(l) * t
                    if is_rgcn(l):
                        act.wait_ge(zact_mm, q + 1)
                        act.activation(gates[0:P, t % 2, :], ps[0:P, 2 + q % 2, 0:2], ACT.Sigmoid).then_inc(zact_out, 1)
                        act.wait_ge(zact_out, q + 1)
                        q += 1
                    for r in range(2 if is_rgcn(l) else 1):
                        act.wait_ge(zact_mm, q + 1)
                        bank = ps[0:P, 2 + q % 2, :]
                        if is_conv(l):
                            act.activation(zfull[0:P, t, :], bank, ACT.Copy).then_inc(zact_out, 1)
                        elif l == GAT:
                            act.activation(hh[0:P, t, :, 0:LAT], bank.rearrange("p (h f) -> p h f", h=HEADS), ACT.Copy).then_inc(zact_out, 1)
                        else:
                            scale = gates[0:P, t % 2, r:r + 1] if is_rgcn(l) else 1.0
                            if s >= 2:
                                act.wait_ge(split_done, s - 1)
                            act.activation(zt[0:P, s % 2], bank, ACT.Copy, scale=scale)
                            act.activation(parts[0:P, r, 0, t, :], bank, ACT.Copy, scale=scale).then_inc(zact_out, 1)
                            s += 1
                        q += 1

            empty_groups(RGCN0)

            def empty_pair(m):
                qd, qp = divmod(m, NT // 2)
                act.wait_ge(hot_used, m + 1)
                bank = 2 * m % 8

                def blk(v):
                    return ps[0:P, bank:bank + 2, v * P:(v + 1) * P]

                act.activation(adj[0:P, 1, qd, 2 * qp * P:2 * (qp + 1) * P].rearrange("p (n c) -> p n c", n=2), blk(1), ACT.Copy)
                if qp == 0 and qd >= 2:
                    act.wait_ge(stage_out[qd % 2], 32 * (qd // 2))
                act.activation(stage_c[0:P, qd % 2, 2 * qp:2 * qp + 2, :], blk(2), ACT.Copy)
                act.activation(stage_w[0:P, qd % 2, 2 * qp:2 * qp + 2, :], blk(3), ACT.Copy).then_inc(pair_act, 1)

            general = overflowed(act)
            with act.If(general == 0):
                for m in range(BUCKETS // 2):
                    empty_pair(m)

            for l in LAYERS[1:]:
                empty_groups(l)
                if l in (RGCN1, CONV1, SAGE2):
                    blk0 = NT * (RGCN1, CONV1, SAGE2).index(l)
                    for t in range(NT):
                        std(blk0 + t)
            empty_groups(GAT)
            for n in range(2):
                act.wait_ge(score_tr, n + 1)
                if n:
                    act.wait_ge(rows_stored, 16 * NT)
                act.activation(score_rows, ps[0:8 * NT, 6, 0:P], ACT.Copy).then_inc(score_row, 1)

            def below_pos(i):
                h, k = divmod(i, NT)
                if k == 0:
                    act.wait_ge(headrow_in[h % 2], 32 * (h // 2 + 1))
                if i >= 3:
                    act.wait_ge(attn, i - 2)
                if not i % 2:
                    act.activation(neg_t[0:P, i // 2 % 2], head_rows[0:P, h % 2, 1, :], ACT.Relu, bias=minus_slope_dst[0:P, k, h:h + 1])
                act.activation(pos_t[0:P, i % 3], head_rows[0:P, h % 2, 0, :], ACT.Relu, bias=minus_dst[0:P, k, h:h + 1]).then_inc(pos_ready, 1)

            act.wait_ge(score_ready, NT + 1)
            below_pos(0)
            below_pos(1)
            for i in range(HEADS * NT):
                act.wait_ge(below, i + 1)
                act.activation(pos_t[0:P, i % 3], pos_t[0:P, i % 3], ACT.Exp, scale=-1.0).then_inc(expd, 1)
                if i + 2 < HEADS * NT:
                    below_pos(i + 2)

        @block.vector
        def _(dve):
            steps = [0]

            def step(ins):
                steps[0] += 1
                ins.then_inc(dve_step, 1)
                dve.wait_ge(dve_step, steps[0])

            dve.wait_ge(const_ready, 6)
            dve.wait_ge(edge_in, 64)
            sd, quo, low = rk[0:P, 640:960], rk[0:P, 960:1280], rk[0:P, 1280:1600]
            dve.tensor_copy(sd, rk[0:P, 0:320].bitcast(I32))
            step(dve.tensor_scalar(rec[:, :, 2], rk[0:P, 320:480].bitcast(I32), 0, None, ALU.not_equal))
            step(dve.tensor_scalar(quo, sd, float(P), None, ALU.is_ge))
            for k in range(2, NT):
                step(dve.scalar_tensor_tensor(quo, sd, float(k * P), quo, ALU.is_ge, ALU.add))
            step(dve.scalar_tensor_tensor(low, quo, -float(P), sd, ALU.mult, ALU.add))
            dve.tensor_copy(rec[:, :, 0], low[:, 0:EC])
            dve.tensor_copy(rec[:, :, 1], low[:, EC:2 * EC])
            dve.tensor_copy(rec[:, :, 3], rk[0:P, 480:640])
            step(dve.scalar_tensor_tensor(bucket, quo[:, EC:2 * EC], float(NT), quo[:, 0:EC], ALU.mult, ALU.add))
            for b in range(BUCKETS):
                last = dve.tensor_scalar(hot[:, b, :], bucket, float(b), 0.0, ALU.is_equal, ALU.add, accum_out=totals[:, b:b + 1])
            last.then_inc(totals_ready, 1)
            dve.wait_ge(prefix_ready, 1)
            dve.tensor_copy(before, ps[0:P, 4, 0:BUCKETS])
            step(dve.tensor_reduce(fullest[:, :], ps[:, 4, 128:128 + BUCKETS], AX.X, ALU.max))
            dve.tensor_scalar(overflow[:, :], fullest[:, :], CAP + 0.5, None, ALU.is_ge).then_inc(overflow_ready, 1)
            for b in range(BUCKETS):
                last = dve.tensor_tensor_scan(running[:, b, :], ones_bf[0:P, :], hot[:, b, :], before[:, b:b + 1], ALU.mult, ALU.add)
            step(last)
            step(dve.tensor_tensor(running, running, hot, ALU.mult))
            step(dve.tensor_reduce(rank, running.rearrange("p b c -> p c b"), AX.X, ALU.add))
            step(dve.tensor_scalar(high, rank, 128.5, -float(128 * CHUNKS - 1), ALU.is_ge, ALU.mult))
            step(dve.scalar_tensor_tensor(high, bucket, 2.0, high, ALU.mult, ALU.add))
            step(dve.tensor_scalar(rank, rank, -1.0, float(CHUNKS), ALU.add, ALU.mult))
            step(dve.tensor_tensor(rank, rank, high, ALU.add))
            dve.tensor_copy(slot, rank).then_inc(slots_ready, 1)

            def norm_relu(q, xt, ht):
                step(dve.bn_stats(stats[0:P, :], xt))
                dve.bn_aggr(mv[0:P, 0:2], stats[0:P, :]).then_inc(var_ready, 1)
                dve.wait_ge(std_ready, q + 1)
                step(dve.reciprocal(mv[0:P, 3:4], mv[0:P, 2:3]))
                step(dve.tensor_scalar(ht, xt, mv[0:P, 0:1], mv[0:P, 3:4], ALU.subtract, ALU.mult))
                dve.tensor_scalar(ht, ht, 0.0, None, ALU.max).then_inc(h_ready, 1)

            dve.wait_ge(first_x_in, 16)
            for t in range(NT):
                last = dve.bn_stats(first_stats[:, t, :], h_all[0:P, t])
            step(last)
            for t in range(NT):
                last = dve.bn_aggr(first_mv[:, t, 0:2], first_stats[:, t, :])
            last.then_inc(first_var, 1)
            dve.wait_ge(first_std, 1)
            step(dve.reciprocal(first_mv[:, :, 3], first_mv[:, :, 2]))
            for t in range(NT):
                last = dve.tensor_scalar(h_all[0:P, t], h_all[0:P, t], first_mv[:, t, 0:1], first_mv[:, t, 3:4], ALU.subtract, ALU.mult)
            step(last)
            for t in range(NT):
                dve.tensor_scalar(h_all[0:P, t], h_all[0:P, t], 0.0, None, ALU.max).then_inc(h_ready, 1)

            dve.wait_ge(node_in, 16)

            def self_terms_and_splits(l):
                s = splits_before(l)
                dve.wait_ge(weights_in, 16 * loads_before(l + 1))
                for t in range(NT):
                    q = z_before(l, act_groups) + act_groups(l) * t
                    for r in range(0 if is_conv(l) else 2 if is_rgcn(l) else 1):
                        dve.wait_ge(zact_out, q + (2 if is_rgcn(l) else 1) + r)
                        step(dve.tensor_tensor(zt[0:P, s % 2], zt[0:P, s % 2], parts[0:P, r, 0, t, :], ALU.subtract))
                        step(dve.tensor_copy(parts[0:P, r, 1, t, :], zt[0:P, s % 2]))
                        dve.tensor_tensor(parts[0:P, r, 2, t, :], zt[0:P, s % 2], parts[0:P, r, 1, t, :], ALU.subtract).then_inc(split_done, 1)
                        s += 1
                    qv = z_before(l, vec_groups) + t
                    dve.wait_ge(zvec_mm, qv + 1)
                    bank = ps[0:P, 4 + qv % 2, :]
                    if is_conv(l):
                        dve.scalar_tensor_tensor(selfs[0:P, t], bank, node_scale[0:P, t:t + 1], bias[0:P, l % 2, :],
                                                 ALU.mult, ALU.add).then_inc(zvec_out, 1)
                    else:
                        dve.tensor_tensor(selfs[0:P, t], bank, bias[0:P, l % 2, :], ALU.add).then_inc(zvec_out, 1)

            def epilogue(l, t):
                g = NT * l + t
                dve.wait_ge(agg_mm, g + 1)
                bank = ps[0:P, 6 + g % 2, :]
                tmp = ht_tmp[0:P, t % 2]
                if is_sage(l):
                    ins = dve.scalar_tensor_tensor(tmp, bank, inv_deg[0:P, t:t + 1], selfs[0:P, t], ALU.mult, ALU.add)
                else:
                    ins = dve.tensor_tensor(tmp, bank, selfs[0:P, t], ALU.add)
                ins.then_inc(agg_out, 1)
                dve.wait_ge(agg_out, g + 1)
                if l in (RGCN0, CONV0, SAGE0, SAGE1):
                    dve.tensor_scalar(h_all[0:P, t], tmp, 0.0, None, ALU.max).then_inc(h_ready, 1)
                    return
                q = NT * (RGCN1, CONV1, SAGE2).index(l) + t
                x = xin[0:P, q % 2]
                dve.wait_ge(x_in[q % 2], 16 * (q // 2 + 1))
                if l == CONV1:
                    dve.wait_ge(hin_in[t % 2], 16 * (t // 2 + 1))
                    step(dve.scalar_tensor_tensor(tmp, tmp, 0.0, hin[0:P, t % 2], ALU.max, ALU.add))
                    step(dve.scalar_tensor_tensor(x, tmp, 0.5, x, ALU.mult, ALU.add))
                else:
                    step(dve.tensor_tensor(x, x, tmp, ALU.add))
                norm_relu(q, x, h_all[0:P, t])
                dve.engine_nop().then_inc(x_ready, 1)

            def add_rests(l):
                if is_conv(l):
                    return
                rels = 2 if is_rgcn(l) else 1
                first = rest_before(l) + (NT if l == SAGE0 else 0)
                with dve.If(general != 0):
                    for t in range(NT):
                        dve.wait_ge(rest_used, first + (t + 1) * rels)
                        if is_sage(l):
                            dve.scalar_tensor_tensor(selfs[0:P, t], ps[0:P, 6, :], inv_deg[0:P, t:t + 1], selfs[0:P, t], ALU.mult, ALU.add).then_inc(rest_out, 1)
                        else:
                            dve.tensor_tensor(selfs[0:P, t], ps[0:P, 6, :], selfs[0:P, t], ALU.add).then_inc(rest_out, 1)
                    dve.wait_ge(rest_out, rest_tiles_before(l) + NT)

            self_terms_and_splits(RGCN0)

            def all_edges():
                dve.wait_ge(raw_ready, 64)
                started = [0]

                def first(ins):
                    started[0] += 1
                    ins.then_inc(raw_step, 1)
                    dve.wait_ge(raw_step, started[0])

                wbf, wrest = ht_tmp[0:P, 0, 0:EC // 2].bitcast(BF16), ht_tmp[0:P, 1, 0:EC]
                w = raw_in[:, 3 * EC:]
                first(dve.tensor_copy(raw_node.rearrange("p v c -> p (v c)"), raw_in[:, 0:2 * EC].bitcast(I32)))
                first(dve.tensor_scalar(raw_type[:, 0, :], raw_in[:, 2 * EC:3 * EC].bitcast(I32), 0, None, ALU.is_equal))
                first(dve.tensor_scalar(raw_type[:, 1, :], raw_in[:, 2 * EC:3 * EC].bitcast(I32), 0, None, ALU.not_equal))
                first(dve.tensor_scalar(tile_base, iota_c[0:P, 0:NT], float(P), None, ALU.mult))
                first(dve.tensor_copy(wbf, w))
                first(dve.tensor_copy(raw_w[:, 0, :], wbf))
                first(dve.tensor_tensor(wrest, w, raw_w[:, 0, :], ALU.subtract))
                first(dve.tensor_copy(wbf, wrest))
                first(dve.tensor_copy(raw_w[:, 1, :], wbf))
                first(dve.tensor_tensor(raw_w[:, 2, :], wrest, raw_w[:, 1, :], ALU.subtract))
                per_pair = 4 + 3 * 2 + 1
                dve.engine_nop().then_inc(chunk_hot, 1)
                dve.engine_nop().then_inc(chunk_used, 1)
                dve.engine_nop().then_inc(pair_vec, 1)
                with dve.Fori(0, NT) as qd:
                    with dve.Fori(0, NT // 2) as qp:
                        done = [0]

                        def mark(ins):
                            done[0] += 1
                            ins.then_inc(raw_step, 1)

                        def wait_marks():
                            dve.wait_ge(raw_step, started[0] + (5 * qd + qp) * per_pair + done[0])

                        for bb in range(2):
                            dve.wait_ge(chunk_hot, (10 * qd + 2 * qp + bb) * EC + 1)
                            mark(dve.tensor_scalar(rel_node[:, 0, :], raw_node[:, 0, :], tile_base[:, bass.ds(2 * qp + bb, 1)], None, ALU.subtract))
                            mark(dve.tensor_scalar(rel_node[:, 1, :], raw_node[:, 1, :], tile_base[:, bass.ds(qd, 1)], None, ALU.subtract))
                            with dve.Fori(0, EC) as c:
                                wait_marks()
                                dve.wait_ge(chunk_used, (10 * qd + 2 * qp + bb) * EC + c + 1)
                                src, dst = rel_node[:, 0, bass.ds(c, 1)], rel_node[:, 1, bass.ds(c, 1)]
                                dve.tensor_scalar(onehots[0:P, 0, 0, :], iota_c[0:P, :], src, None, ALU.is_equal)
                                dve.tensor_scalar(onehots[0:P, 0, 1, :], iota_c[0:P, :], dst, None, ALU.is_equal)
                                for s in range(3):
                                    dve.tensor_scalar(onehots[0:P, 0, 2 + s, :], iota_c[0:P, :], dst, raw_w[:, s, bass.ds(c, 1)], ALU.is_equal, ALU.mult)
                                dve.tensor_scalar(onehots[0:P, 0, 5, :], iota_c[0:P, :], dst, raw_type[:, 1, bass.ds(c, 1)], ALU.is_equal, ALU.mult)
                                dve.tensor_scalar(onehots[0:P, 1, 0, :], iota_c[0:P, :], dst, raw_type[:, 0, bass.ds(c, 1)], ALU.is_equal, ALU.mult).then_inc(chunk_hot, 1)
                        dve.wait_ge(chunk_used, (10 * qd + 2 * qp + 2) * EC + 1)

                        def blk(v):
                            return ps[0:P, 0:2, v * P:(v + 1) * P]

                        def cols(ap):
                            return ap[:, bass.ds(qp * (2 * P), 2 * P)].rearrange("p (n c) -> p n c", n=2)

                        total = cols(stage_w[0:P, 1].rearrange("p k c -> p (k c)"))
                        for v in range(3):
                            if v < 2:
                                near = cols(adj[0:P, v, bass.ds(qd, 1), :].rearrange("p o n -> p (o n)"))
                                rest = cols(rest_row[:, v, :])
                            else:
                                near = cols(stage_c[0:P, 0].rearrange("p k c -> p (k c)"))
                                rest = cols(stage_c[0:P, 1].rearrange("p k c -> p (k c)"))
                            mark(dve.tensor_copy(near, blk(v)))
                            wait_marks()
                            mark(dve.tensor_tensor(rest, blk(v), near, ALU.subtract))
                        mark(dve.tensor_copy(total, blk(0)))
                        wait_marks()
                        dve.tensor_tensor(total, total, blk(1), ALU.add)
                        dve.tensor_copy(cols(stage_w[0:P, 0].rearrange("p k c -> p (k c)")), blk(3)).then_inc(pair_vec, 1)
                    dve.wait_ge(row_stored, 96 * qd + 96)

            def untyped_pair(m):
                qd, qp = divmod(m, NT // 2)
                bank = 2 * m % 8
                dve.wait_ge(pair_act, m + 1)
                at = (slice(0, P), slice(None))
                cols = slice(2 * qp * P, 2 * (qp + 1) * P)
                dve.tensor_tensor(adj[0:P, 0, qd, cols].rearrange("p (n c) -> p n c", n=2), ps[0:P, bank:bank + 2, 0:P],
                                  adj[0:P, 1, qd, cols].rearrange("p (n c) -> p n c", n=2), ALU.subtract).then_inc(pair_vec, 1)

            general = overflowed(dve)
            steps_before = steps[0]
            with dve.If(general == 0):
                dve.wait_ge(table_in, 16)
                dve.tensor_copy(iota4, iota_c[:, :].unsqueeze(2).broadcast_to([128, 128, 4]))
                dve.tensor_copy(node_bf, table[:, :, 0:2].rearrange("p j v -> p v j"))
                dve.tensor_copy(coef_bf[:, 3, :], table[:, :, 2])
                wrest = ht_tmp[:, 0, 0:CHUNKS]
                step(dve.tensor_copy(coef_bf[:, 0, :], table[:, :, 3]))
                step(dve.tensor_tensor(wrest, table[:, :, 3], coef_bf[:, 0, :], ALU.subtract))
                step(dve.tensor_copy(coef_bf[:, 1, :], wrest))
                step(dve.tensor_tensor(coef_bf[:, 2, :], wrest, coef_bf[:, 1, :], ALU.subtract))
                for m in range(BUCKETS // 2):
                    if m >= 4:
                        dve.wait_ge(hot_used, m - 3)
                    hots = pair_hot(m)
                    chunks = slice(4 * m, 4 * m + 4)
                    step(dve.tensor_tensor(hots[:, 0:2], iota4.unsqueeze(1).broadcast_to([128, 2, 128, 4]),
                                           node_bf[:, :, chunks].unsqueeze(2).broadcast_to([128, 2, 128, 4]), ALU.is_equal))
                    dve.tensor_tensor(hots[:, 2:6], hots[:, 1:2].broadcast_to([128, 4, 128, 4]),
                                      coef_bf[:, :, chunks].unsqueeze(2).broadcast_to([128, 4, 128, 4]), ALU.mult).then_inc(hot_ready, 1)
                    if m >= 2:
                        untyped_pair(m - 2)
                untyped_pair(BUCKETS // 2 - 2)
                untyped_pair(BUCKETS // 2 - 1)
                for n in range(2):
                    dve.wait_ge(stage_out[n], 16 * NT)
            with dve.Else():
                dve.engine_nop().then_inc(dve_step, steps[0] - steps_before)
                all_edges()

            add_rests(RGCN0)
            wait_tiles(dve, NT)
            for t in range(NT):
                for n in range(6 * t, 6 * t + 6):
                    b, kh = divmod(n, 2)
                    dve.wait_ge(basis2_in[n % 2], 16 * (n // 2 + 1))
                    if n >= 2:
                        dve.wait_ge(basis2_used, n - 1)
                    for r in range(2):
                        w = wts[:, r, 2 * kh:2 * kh + 2, :]
                        coef = att[:, 1, r * BASES + b:r * BASES + b + 1]
                        if b == 0:
                            last = dve.tensor_scalar(w, basis2_ring[:, n % 2], coef, None, ALU.mult)
                        else:
                            last = dve.scalar_tensor_tensor(w, basis2_ring[:, n % 2], coef, w, ALU.mult, ALU.add)
                    last.then_inc(basis2_used, 1)
                epilogue(RGCN0, t)
            dve.wait_ge(basis2_used, 2 * BASES)
            dve.engine_nop().then_inc(w2_ready, 1)

            for l in LAYERS[1:]:
                self_terms_and_splits(l)
                if l == CONV0:
                    dve.wait_ge(hin_stored, 16 * NT)
                if l == SAGE0:
                    dve.wait_ge(deg_mm, 1)
                    step(dve.tensor_copy(inv_deg[0:P, :], ps[0:P, 6, 0:NT]))
                    with dve.If(general != 0):
                        dve.wait_ge(rest_used, rest_before(l) + NT)
                        dve.tensor_tensor(inv_deg[0:P, :], inv_deg[0:P, :], ps[0:P, 7, 0:NT], ALU.add).then_inc(rest_degree, 1)
                        dve.wait_ge(rest_degree, 1)
                    step(dve.tensor_scalar(inv_deg[0:P, :], inv_deg[0:P, :], 1.0, None, ALU.max))
                    dve.reciprocal(inv_deg[0:P, :], inv_deg[0:P, :]).then_inc(deg_out, 1)
                    dve.wait_ge(deg_out, 1)
                add_rests(l)
                for t in range(NT):
                    epilogue(l, t)
                if l == SAGE1:
                    dve.wait_ge(typed_in, 32)
                    dve.tensor_tensor(adj[0:P, 1], adj[0:P, 1], type1_in, ALU.add).then_inc(gat_typed, 1)

            dve.wait_ge(weights_in, 16 * (loads_before(GAT + 1) + 2))
            for t in range(NT):
                dve.wait_ge(zact_out, z_before(GAT, act_groups) + t + 1)
                for v in range(2):
                    prod = ht_tmp[0:P, v].rearrange("p (h f) -> p h f", h=HEADS)
                    step(dve.tensor_tensor(prod, hh[0:P, t, :, 0:LAT], a_both[0:P, v].rearrange("p (h f) -> p h f", h=HEADS), ALU.mult))
                    last = dve.tensor_reduce(score[0:P, t, 4 * v:4 * v + 4], prod, AX.X, ALU.add)
                last.then_inc(score_ready, 1)
            dve.wait_ge(adrow_in, 16 * HEADS)
            for t in range(NT):
                step(dve.tensor_scalar(pos_t[0:P, 0].rearrange("p (k c) -> p k c", k=NT), adj[0:P, 0, :, t * P:(t + 1) * P],
                                       0.0, NEG, ALU.is_equal, ALU.mult))
                for h in range(HEADS):
                    step(dve.tensor_tensor_reduce(attn_t[0:P, 0], pos_t[0:P, 0], ad_rows[0:P, h, :], 1.0, NEG,
                                                  ALU.add, ALU.max, top[0:P, t, h:h + 1]))
            dve.wait_ge(gat_in, 2)
            step(dve.tensor_tensor(top[0:P], top[0:P], score[0:P, :, 4:8], ALU.add))
            step(dve.scalar_tensor_tensor(top[0:P], top[0:P], SLOPE, top[0:P], ALU.mult, ALU.max))
            dve.tensor_scalar(minus_dst[0:P], score[0:P, :, 0:4], -1.0, None, ALU.mult)
            dve.tensor_scalar(minus_slope_dst[0:P], score[0:P, :, 0:4], -SLOPE, None, ALU.mult)
            dve.tensor_tensor(score2[0:P, :, 0:4], top[0:P], score[0:P, :, 4:8], ALU.subtract)
            dve.scalar_tensor_tensor(score2[0:P, :, 4:8], score[0:P, :, 4:8], -SLOPE, top[0:P], ALU.mult, ALU.add).then_inc(score_ready, 1)

            def finish_head(h):
                dve.wait_ge(attn_used, NT * (h + 1))
                b0 = 4 * (h % 2)
                den = ps[0:P, b0:b0 + 3, 0:3 * (LAT + 1)].rearrange("p n (c f) -> p n c f", c=3)[:, :, :, LAT]
                step(dve.tensor_scalar(rden[0:P, 0:9].rearrange("p (n c) -> p n c", n=3), den, 1e-30, None, ALU.max))
                step(dve.tensor_scalar(rden[0:P, 9:10], ps[0:P, b0 + 3, LAT:LAT + 1], 1e-30, None, ALU.max))
                step(dve.reciprocal(rden[0:P], rden[0:P]))
                for t in range(NT):
                    c0 = (t % 3) * (LAT + 1)
                    x = selfs[0:P, t, h * LAT:(h + 1) * LAT]
                    last = dve.scalar_tensor_tensor(x, ps[0:P, b0 + t // 3, c0:c0 + LAT], rden[0:P, t:t + 1], x, ALU.mult, ALU.add)
                last.then_inc(head_out, 1)

            dve.wait_ge(gat_typed, 1)
            dve.wait_ge(x3_in, 16)
            def smaller(i):
                h, k = divmod(i, NT)
                if i % 2:
                    dve.tensor_scalar(neg_vec, head_rows[0:P, h % 2, 1, :], minus_slope_dst[0:P, k, h:h + 1], 0.0,
                                      ALU.add, ALU.max).then_inc(neg_ready, 1)
                    dve.wait_ge(neg_ready, i // 2 + 1)
                dve.wait_ge(pos_ready, i + 1)
                neg = neg_vec if i % 2 else neg_t[0:P, i // 2 % 2]
                dve.tensor_tensor(pos_t[0:P, i % 3], pos_t[0:P, i % 3], neg, ALU.min).then_inc(below, 1)

            def attention(count, ready):
                smaller(0)
                for i in range(HEADS * NT):
                    if i + 1 < HEADS * NT:
                        smaller(i + 1)
                    dve.wait_ge(expd, i + 1)
                    if i >= 2:
                        dve.wait_ge(attn_used, i - 1)
                    ready(i)
                    dve.tensor_tensor(attn_t[0:P, i % 2], pos_t[0:P, i % 3], count(i), ALU.mult).then_inc(attn, 1)
                    if i % NT == 1 and i > NT:
                        finish_head(i // NT - 1)
                finish_head(HEADS - 1)

            steps_before = steps[0]
            with dve.If(general == 0):
                attention(lambda i: adj[0:P, 1, i % NT, :], lambda i: None)
            with dve.Else():
                steps[0] = steps_before
                attention(lambda i: total_row, lambda i: dve.wait_ge(total_in, 16 * (i + 1)))


_INS = ["x", "src", "dst", "edge_type_2", "edge_weight", "node_vec",
        "L0_gnn_basis1", "L0_gnn_att1", "L0_gnn_gate_w1", "L0_gnn_root1", "L0_gnn_bias1",
        "L0_gnn_basis2", "L0_gnn_att2", "L0_gnn_gate_w2", "L0_gnn_root2", "L0_gnn_bias2",
        "L1_gnn_W0_1", "L1_gnn_W1_1", "L1_gnn_b1", "L1_gnn_W0_2", "L1_gnn_W1_2", "L1_gnn_b2",
        "L2_gnn_Ws_self", "L2_gnn_Ws_neigh", "L2_gnn_bs", "L3_gnn_W", "L3_gnn_a"]


def kernel(**inputs):
    import concourse.bacc as bacc
    from concourse.bass_utils import run_bass_kernel_spmd as run

    nc = bacc.Bacc("TRN2", target_bir_lowering=False, num_devices=1)
    arrays, args = {}, {}
    for name in _INS:
        arr = np.ascontiguousarray(inputs[name])
        arrays[f"in_{name}"] = arr
        args[name] = nc.dram_tensor(f"in_{name}", arr.shape, mybir.dt.from_np(arr.dtype), kind="ExternalInput").ap()
    out = nc.dram_tensor("out_x", (NODES, H), F32, kind="ExternalOutput").ap()
    build(nc, args, out)
    r = run(nc, [arrays], core_ids=[0])
    return r.results[0]["out_x"]
```

```python
from contextlib import ExitStack

import numpy as np

import concourse.bass as bass
from concourse import mybir

F32 = mybir.dt.float32
BF16 = mybir.dt.bfloat16
I32 = mybir.dt.int32
ALU = mybir.AluOpType
ACT = mybir.ActivationFunctionType
AX = mybir.AxisListType

NODES, H, EDGES, HEADS, LAT = 1250, 512, 20000, 4, 128
P = 125
NT = NODES // P
KT = H // 128
EC = EDGES // P
BUCKETS = NT * NT
CAP = 256
SLOTS = BUCKETS * CAP
CHUNKS = SLOTS // 128
BASES = 30
LN_EPS = 1e-5
NEG = -3.0e38
SLOPE = 0.2

RGCN0, RGCN1, CONV0, CONV1, SAGE0, SAGE1, SAGE2, GAT = range(8)
LAYERS = [RGCN0, RGCN1, CONV0, CONV1, SAGE0, SAGE1, SAGE2]


def is_rgcn(l):
    return l in (RGCN0, RGCN1)


def is_conv(l):
    return l in (CONV0, CONV1)


def is_sage(l):
    return l in (SAGE0, SAGE1, SAGE2)


def act_groups(l):
    return 3 if is_rgcn(l) else 1


def vec_groups(l):
    return 0 if l == GAT else 1


def build(nc, a, out):
    ctx = ExitStack()
    with ctx:
        def sb(name, shape, dt=F32):
            return ctx.enter_context(nc.sbuf_tensor(name, shape, dt))

        def sem(name):
            return ctx.enter_context(nc.semaphore(name))

        def scratch(name, shape, dt):
            return nc.dram_tensor(name, shape, dt, kind="Internal").ap()

        table_d = scratch("edge_table", [SLOTS, 4], F32)
        weight_d = scratch("adj_weight", [NT, P, NODES], F32)
        count_d = scratch("adj_count", [P, NT, NODES], BF16)
        typed_d = scratch("adj_typed", [P, 2, NT, NODES], BF16)
        count_rest_d = scratch("count_rest", [P, NT, NODES], BF16)
        typed_rest_d = scratch("typed_rest", [P, 2, NT, NODES], BF16)
        total_d = scratch("count_total", [P, NT, NODES], F32)
        x_d = scratch("x_resid", [3, NODES, H], F32)
        hin_d = scratch("conv_in", [NODES, H], F32)
        rows_d = scratch("gat_rows", [2, 8, NODES], F32)

        big = sb("big", [128, 12500 + NT * H])
        adj = big[:, 0:12500].bitcast(BF16).rearrange("p (r k n) -> p r k n", r=2, k=NT)
        selfs = big[:, 12500:].rearrange("p (t f) -> p t f", t=NT)
        running = big[0:P, 0:BUCKETS * EC].rearrange("p (b c) -> p b c", b=BUCKETS)
        zr = sb("zr", [128, 15360])
        parts = zr[:, :].bitcast(BF16).rearrange("p (r s k f) -> p r s k f", r=2, s=3, k=NT)
        zfull = zr[:, 0:NT * H].rearrange("p (k f) -> p k f", k=NT)
        hot = zr[0:P, 0:8000].bitcast(BF16).rearrange("p (b c) -> p b c", b=BUCKETS)
        basis_ring = zr[:, 8000:8000 + 4096].rearrange("p (n k f) -> p n k f", n=4, k=2)
        rk = zr[:, 12096:15360]
        h_all = sb("h_all", [128, NT, H])
        stage_w = h_all[:, 0:5, :].rearrange("p a b -> p (a b)")[:, 0:2500].rearrange("p (n k c) -> p n k c", n=2, k=NT)
        stage_c = h_all[:, 5:8, :].rearrange("p a b -> p (a b)")[:, 0:1250].bitcast(BF16).rearrange("p (n k c) -> p n k c", n=2, k=NT)
        wts = sb("wts", [128, 3, KT, H])
        hT = sb("hT", [128, 2, KT, P])
        bias = sb("bias", [128, 2, H])
        work = sb("work", [128, 8, H])
        zt = work[:, 0:2]
        xin = work[:, 2:4]
        hin = work[:, 4:6]
        ht_tmp = work[:, 6:8]
        onehots = work[:, :, :].rearrange("p a b -> p (a b)").bitcast(BF16)[:, 0:2 * 6 * 128].rearrange("p (n v c) -> p n v c", n=2, v=6)
        edges = sb("edges", [128, 2240])
        rec = edges[0:P, 0:640].rearrange("p (c f) -> p c f", f=4)
        slot = edges[0:P, 640:800].bitcast(I32)
        table = edges[:, 800:1600].rearrange("p (j f) -> p j f", f=4)
        iota4 = edges[:, 0:256].bitcast(BF16).rearrange("p (c j) -> p c j", j=4)
        node_bf = edges[:, 1600:1800].bitcast(BF16).rearrange("p (v j) -> p v j", v=2)
        coef_bf = edges[:, 1800:2200].bitcast(BF16).rearrange("p (v j) -> p v j", v=4)
        early_sum = big[:, 0:4096].rearrange("p (r k f) -> p r k f", r=2, k=KT)
        early_ring = big[:, 4096:8192].rearrange("p (n k f) -> p n k f", n=4, k=2)
        basis2_ring = edges[:, 0:2048].rearrange("p (n k f) -> p n k f", n=2, k=2)
        raw_in = edges[0:P, 0:640]
        raw_node = edges[0:P, 640:960].rearrange("p (v c) -> p v c", v=2)
        raw_type = edges[0:P, 960:1280].rearrange("p (v c) -> p v c", v=2)
        raw_w = edges[0:P, 1280:1760].rearrange("p (s c) -> p s c", s=3)
        rel_node = edges[0:P, 1760:2080].rearrange("p (v c) -> p v c", v=2)
        tile_base = edges[0:P, 2080:2080 + NT]
        rest_row = work[:, :, :].rearrange("p a b -> p (a b)")[0:P, 1024:1024 + NODES].bitcast(BF16).rearrange("p (v c) -> p v c", v=2)
        ident = sb("ident", [128, 128])
        hT_flat = hT[:, :, :, :].rearrange("p a k c -> p (a k c)")
        diag = hT_flat[:, 0:512].rearrange("p (n c) -> p n c", n=4)
        tri = hT_flat[:, 512:640]
        ones_f = hT_flat[:, 640:768]
        rest_slab = hT_flat[0:P, 0:625].bitcast(BF16).rearrange("p (k c) -> p k c", k=NT)
        iota_c = sb("iota_c", [128, 128], BF16)
        ones_bf = sb("ones_bf", [128, EC], BF16)
        att = sb("att", [128, 2, 2 * BASES])
        gate_w = sb("gate_w", [128, 2, KT, 2])
        gates = sb("gates", [128, 2, 2])
        score_w = sb("score_w", [128, KT, 8])
        node_scale = sb("node_scale", [128, NT])
        inv_deg = sb("inv_deg", [128, NT])
        stats = sb("stats", [128, 6])
        mv = sb("mv", [128, 4])
        eps = sb("eps", [128, 1])
        fullest = sb("fullest", [128, 1])
        overflow = sb("overflow", [128, 1], I32)

        ps = ctx.enter_context(nc.psum_tensor("ps", [128, 8, 512], F32))

        const_ready = sem("const_ready")
        edge_in = sem("edge_in")
        dve_step = sem("dve_step")
        pool_step = sem("pool_step")
        totals_ready = sem("totals_ready")
        prefix_ready = sem("prefix_ready")
        slots_ready = sem("slots_ready")
        table_clear = sem("table_clear")
        scattered = sem("scattered")
        overflow_ready = sem("overflow_ready")
        raw_ready = sem("raw_ready")
        raw_step = sem("raw_step")
        chunk_hot = sem("chunk_hot")
        chunk_used = sem("chunk_used")
        row_stored = sem("row_stored")
        rest_in = sem("rest_in")
        rest_used = sem("rest_used")
        rest_out = sem("rest_out")
        rest_degree = sem("rest_degree")
        total_in = sem("total_in")
        table_in = sem("table_in")
        att_in = sem("att_in")
        basis_in = [sem(f"basis_in{n}") for n in range(4)]
        basis_used = sem("basis_used")
        basis2_in = [sem(f"basis2_in{n}") for n in range(4)]
        basis2_used = sem("basis2_used")
        sum_moved = sem("sum_moved")
        diag_ready = sem("diag_ready")
        combined_out = sem("combined_out")
        first_x_in = sem("first_x_in")
        first_var = sem("first_var")
        first_std = sem("first_std")
        x_in = [sem(f"x_in{n}") for n in range(2)]
        x_ready = sem("x_ready")
        var_ready = sem("var_ready")
        std_ready = sem("std_ready")
        hin_in = [sem(f"hin_in{n}") for n in range(2)]
        weights_in = sem("weights_in")
        w2_ready = sem("w2_ready")
        node_in = sem("node_in")
        h_ready = sem("h_ready")
        transposed = sem("transposed")
        hT_ready = sem("hT_ready")
        zact_mm = sem("zact_mm")
        zact_out = sem("zact_out")
        zvec_mm = sem("zvec_mm")
        zvec_out = sem("zvec_out")
        split_done = sem("split_done")
        agg_mm = sem("agg_mm")
        agg_out = sem("agg_out")
        x_stored = [sem(f"x_stored{n}") for n in range(2)]
        hin_stored = sem("hin_stored")
        nodes_hot = sem("nodes_hot")
        hot_ready = sem("hot_ready")
        hot_used = sem("hot_used")
        pair_act = sem("pair_act")
        pair_typed = sem("pair_typed")
        stage_out = [sem(f"stage_out{n}") for n in range(2)]
        typed_stored = sem("typed_stored")
        count_in = sem("count_in")
        slab_in = [sem(f"slab_in{n}") for n in range(4)]
        deg_mm = sem("deg_mm")
        deg_out = sem("deg_out")
        gat_in = sem("gat_in")
        a_in = sem("a_in")
        score_w_ready = sem("score_w_ready")
        score_mm = sem("score_mm")
        score_row = sem("score_row")
        top_ready = sem("top_ready")
        top_transposed = sem("top_transposed")
        top_row = sem("top_row")
        rows_stored = sem("rows_stored")
        adrow_in = sem("adrow_in")
        headrow_in = [sem(f"headrow_in{n}") for n in range(2)]
        typed_in = sem("typed_in")
        x3_in = sem("x3_in")
        pos_ready = sem("pos_ready")
        neg_ready = sem("neg_ready")
        below = sem("below")
        expd = sem("expd")
        attn = sem("attn")
        attn_used = sem("attn_used")
        head_out = sem("head_out")
        stored = sem("stored")
        gat_typed = sem("gat_typed")

        work_flat = work[:, :, :].rearrange("p a b -> p (a b)")
        h_flat = h_all[:, :, :].rearrange("p a b -> p (a b)")
        wts_flat = wts[:, :, :, :].rearrange("p r k f -> p (r k f)")

        def pair_hot(m):
            def view(flat, floats):
                return flat[:, floats].bitcast(BF16).rearrange("p (v c j) -> p v c j", c=128, j=4)

            if m % 3 < 2:
                hots = view(work_flat, slice(1536 * (m % 3), 1536 * (m % 3 + 1)))
                return [hots[:, v] for v in range(6)], hots[:, 0:2], hots[:, 2:6]
            nodes = view(h_flat, slice(8 * H, 9 * H))
            coefs = view(work_flat, slice(3072, 4096))
            return [nodes[:, v] for v in range(2)] + [coefs[:, v] for v in range(4)], nodes, coefs

        def slab(n):
            return big[0:P, 5 * NODES + NODES * (n % 4):5 * NODES + NODES * (n % 4 + 1)]

        bucket = rk[0:P, 1600:1760]
        totals = rk[0:P, 1760:1860]
        before = rk[0:P, 1860:1960]
        rank = rk[0:P, 1960:2120]
        high = rk[0:P, 2120:2280]
        first_stats = rk[0:P, 2280:2280 + 6 * NT].rearrange("p (t v) -> p t v", v=6)
        first_mv = rk[0:P, 2340:2340 + 4 * NT].rearrange("p (t v) -> p t v", v=4)

        hh = zr[:, 0:NT * HEADS * (LAT + 1)].rearrange("p (t h f) -> p t h f", t=NT, h=HEADS)
        z0 = NT * HEADS * (LAT + 1)
        ad_rows = zr[:, z0:z0 + 4 * NODES].rearrange("p (h c) -> p h c", h=HEADS)
        neg_t = zr[:, z0 + 4 * NODES:z0 + 6 * NODES].rearrange("p (n c) -> p n c", n=2)
        attn_t = zr[:, z0 + 6 * NODES:z0 + 8 * NODES].rearrange("p (n c) -> p n c", n=2)
        hT_gat = zr[:, 10360:10360 + H * NT * P // 128].rearrange("p (t k c) -> p t k c", t=NT, k=KT)
        type1_in = zr[0:P, 7680:7680 + 5 * NODES].bitcast(BF16).rearrange("p (k n) -> p k n", k=NT)
        pos_t = h_flat[:, 0:3 * NODES].rearrange("p (n c) -> p n c", n=3)
        total_row = h_flat[0:P, 3 * NODES:4 * NODES]
        head_rows = wts_flat[:, 0:4 * NODES].rearrange("p (n v c) -> p n v c", n=2, v=2)
        top_rows = wts_flat[0:2 * NT, 4 * NODES:4 * NODES + 2 * P].rearrange("p (n c) -> p n c", n=2)
        score_rows = wts[0:8, 1].rearrange("p k f -> p (k f)")[:, 0:NODES]
        neg_vec = work_flat[0:P, 8 * H - NODES:8 * H]
        max_t = edges[0:P, 0:NODES].rearrange("p (k c) -> p k c", k=NT)
        a_both = work[:, 0:2, :]
        rden = work[:, 4, 64:64 + NT]
        minus_slope_dst = work[:, 4, 128:128 + 4 * NT].rearrange("p (t v) -> p t v", v=4)
        minus_dst = work[:, 4, 192:192 + 4 * NT].rearrange("p (t v) -> p t v", v=4)
        score = work[:, 4, 256:256 + 8 * NT].rearrange("p (t v) -> p t v", v=8)
        top = work[:, 4, 336:336 + 4 * NT].rearrange("p (h t) -> p h t", h=HEADS)
        score2 = work[:, 5, 0:8 * NT].rearrange("p (h v t) -> p h v t", h=HEADS, v=2)

        def hT_tile(g):
            return hT[:, g % 2] if g < NT * GAT else hT_gat[:, g - NT * GAT]

        TOP_ROWS_AT = 3

        def vector_neg(i):
            return i >= (HEADS - 2) * NT and i % 2 == 1

        def top_bank(h):
            return 3 if h in (1, 2) else 7

        block = ctx.enter_context(nc.Block())

        def overflowed(eng):
            eng.wait_ge(overflow_ready, 1)
            return eng.value_load(overflow[0:1, 0:1], min_val=0, max_val=1)

        def rest_tiles_before(l):
            return NT * sum(not is_conv(m) for m in range(l))

        def rest_before(l):
            n = NT * sum(2 if is_rgcn(m) else 1 if is_sage(m) else 0 for m in range(l))
            return n + (NT if l > SAGE0 else 0)

        def rows(ap2d, t):
            return ap2d[t * P:(t + 1) * P, :]

        def z_before(l, kind):
            return NT * sum(kind(m) for m in range(l))

        def agg_before(l):
            return NT * l

        def splits_before(l):
            return NT * sum(2 if is_rgcn(m) else 1 if is_sage(m) else 0 for m in range(l))

        def loads_before(l):
            return sum(4 if is_rgcn(m) or m == GAT else 3 for m in range(l))

        def wait_tiles(eng, n):
            if n <= NT * GAT:
                eng.wait_ge(zvec_mm, n)
            else:
                eng.wait_ge(zact_mm, z_before(GAT, act_groups) + n - NT * GAT)

        FIRST_BASIS2 = 38
        BEFORE_Z = 16
        EARLY = BEFORE_Z + 3 * (NT - 1)
        TABLE_AT = EARLY - 5
        FIRST_STD = 46
        NBAS = 2 * BASES

        @block.sync
        def _(sp):
            sp.dma_start(rk[0:P, 0:160].bitcast(I32), a["src"].rearrange("(p c) -> p c", p=P)).then_inc(edge_in, 16)
            sp.dma_start(rk[0:P, 160:320].bitcast(I32), a["dst"].rearrange("(p c) -> p c", p=P)).then_inc(edge_in, 16)
            sp.dma_start(rk[0:P, 320:480].bitcast(I32), a["edge_type_2"].rearrange("(p c) -> p c", p=P)).then_inc(edge_in, 16)
            sp.dma_start(rk[0:P, 480:640], a["edge_weight"].rearrange("(p c) -> p c", p=P)).then_inc(edge_in, 16)
            def load_basis2(n):
                b, kh = divmod(n, 2)
                buffers = 4 if n < EARLY else 2
                if n >= buffers:
                    sp.wait_ge(basis2_used, n - buffers + 1)
                sp.dma_start(early_ring[:, n % 4] if n < EARLY else basis2_ring[:, n % 2],
                             a["L0_gnn_basis2"][b].rearrange("(k p) f -> p k f", p=128)[:, 2 * kh:2 * kh + 2, :]
                             ).then_inc(basis2_in[n % 4], 16)

            for n in range(NBAS):
                kh, b = divmod(n, BASES)
                if n == 8:
                    sp.dma_start(h_all[0:P], a["x"].rearrange("(t p) f -> p t f", p=P)).then_inc(first_x_in, 16)
                if n >= 4:
                    sp.wait_ge(basis_used, n - 3)
                sp.dma_start(basis_ring[:, n % 4],
                             a["L0_gnn_basis1"][b].rearrange("(k p) f -> p k f", p=128)[:, 2 * kh:2 * kh + 2, :]
                             ).then_inc(basis_in[n % 4], 16)
                if n == FIRST_BASIS2:
                    sp.wait_ge(slots_ready, 1)
                if FIRST_BASIS2 <= n < FIRST_BASIS2 + BEFORE_Z:
                    load_basis2(n - FIRST_BASIS2)
            general = overflowed(sp)
            for n in range(BEFORE_Z, EARLY):
                if n == TABLE_AT:
                    sp.wait_ge(scattered, 16 * EC)
                    with sp.If(general == 0):
                        sp.dma_start(table, table_d.rearrange("(p j) f -> p j f", p=128)).then_inc(table_in, 16)
                load_basis2(n)
            with sp.If(general == 0):
                for qd in range(NT):
                    sp.wait_ge(pair_act, 5 * (qd + 1))
                    sp.dma_start(weight_d[qd], stage_w[0:P, qd % 2].rearrange("p k c -> p (k c)")).then_inc(stage_out[qd % 2], 16)
                    sp.dma_start(count_d[:, qd, :], stage_c[0:P, qd % 2].rearrange("p k c -> p (k c)")).then_inc(stage_out[qd % 2], 16)
                for n in range(2):
                    sp.wait_ge(stage_out[n], 16 * NT)
            with sp.Else():
                for n, name in enumerate(("src", "dst", "edge_type_2")):
                    sp.dma_start(raw_in[:, n * EC:(n + 1) * EC].bitcast(I32), a[name].rearrange("(p c) -> p c", p=P)).then_inc(raw_ready, 16)
                sp.dma_start(raw_in[:, 3 * EC:], a["edge_weight"].rearrange("(p c) -> p c", p=P)).then_inc(raw_ready, 16)
                with sp.Fori(0, NT) as qd:
                    sp.wait_ge(pair_typed, 5 * qd + 6)
                    sp.dma_start(weight_d[bass.ds(qd, 1)].rearrange("o p n -> p (o n)"), stage_w[0:P, 0].rearrange("p k c -> p (k c)")).then_inc(row_stored, 16)
                    sp.dma_start(total_d[:, bass.ds(qd, 1), :].rearrange("p o n -> p (o n)"), stage_w[0:P, 1].rearrange("p k c -> p (k c)")).then_inc(row_stored, 16)
                    sp.dma_start(count_d[:, bass.ds(qd, 1), :].rearrange("p o n -> p (o n)"), stage_c[0:P, 0].rearrange("p k c -> p (k c)")).then_inc(row_stored, 16)
                    sp.dma_start(count_rest_d[:, bass.ds(qd, 1), :].rearrange("p o n -> p (o n)"), stage_c[0:P, 1].rearrange("p k c -> p (k c)")).then_inc(row_stored, 16)
                    for r in range(2):
                        sp.dma_start(typed_rest_d[:, r, bass.ds(qd, 1), :].rearrange("p o n -> p (o n)"), rest_row[:, r, :]).then_inc(row_stored, 16)
                sp.wait_ge(row_stored, 96 * NT)

            def load_rests(l, src):
                wait_tiles(sp, NT * (l + 1))
                rels = 2 if is_rgcn(l) else 1
                for n in range(NT * rels if l != SAGE0 else 2 * NT):
                    t, r = divmod(n % NT if l == SAGE0 else n, rels)
                    if rest_before(l) + n:
                        sp.wait_ge(rest_used, rest_before(l) + n)
                    sp.dma_start(rest_slab, src(r, t)).then_inc(rest_in, 16)

            def typed_rest(r, t):
                return typed_rest_d[:, r, :, t * P:(t + 1) * P]

            def count_rest(r, t):
                return count_rest_d[:, t, :].rearrange("p (k c) -> p k c", k=NT)

            sp.wait_ge(pair_typed, NT * NT // 2)
            sp.dma_start(typed_d, adj[0:P]).then_inc(typed_stored, 16)
            with sp.If(general != 0):
                load_rests(RGCN0, typed_rest)
            for n in range(EARLY, NBAS):
                load_basis2(n)
            with sp.If(general != 0):
                load_rests(RGCN1, typed_rest)
            for l in (CONV0, CONV1):
                for t in range(NT):
                    n = (l - CONV0) * NT + t
                    if n == 0:
                        sp.wait_ge(agg_mm, agg_before(CONV0))
                        sp.wait_ge(typed_stored, 16)
                        sp.dma_start(adj[0:P, 0], count_d).then_inc(count_in, 16)
                    if n >= 4:
                        sp.wait_ge(agg_mm, agg_before(CONV0) + n - 3)
                    sp.dma_start(slab(n), weight_d[t]).then_inc(slab_in[n % 4], 16)
            sp.dma_start(type1_in, typed_d[:, 1]).then_inc(typed_in, 16)
            sp.wait_ge(agg_mm, agg_before(SAGE0))
            sp.dma_start(adj[0:P, 1], typed_d[:, 0]).then_inc(typed_in, 16)
            with sp.If(general != 0):
                for l in (SAGE0, SAGE1, SAGE2):
                    load_rests(l, count_rest)
            sp.wait_ge(score_row, 1)
            sp.dma_start(rows_d[0], score_rows).then_inc(rows_stored, 16)
            sp.wait_ge(rows_stored, 16)
            for h in range(HEADS):
                sp.dma_start(ad_rows[:, h, :], rows_d[0, h].partition_broadcast(128)).then_inc(adrow_in, 16)

            def load_head_rows(h):
                sp.wait_ge(top_row, h + 1)
                sp.dma_start(rows_d[1].rearrange("(v h) (t c) -> h v t c", v=2, t=NT)[h], top_rows[:, h % 2, :]).then_inc(rows_stored, 16)
                sp.wait_ge(rows_stored, 16 * (h + 2))
                if h >= 2:
                    sp.wait_ge(expd, NT * (h - 1))
                for v in range(2):
                    sp.dma_start(head_rows[:, h % 2, v, :], rows_d[1, 4 * v + h].partition_broadcast(128)).then_inc(headrow_in[h % 2], 16)

            load_head_rows(0)
            load_head_rows(1)
            with sp.If(general != 0):
                for i in range(HEADS * NT):
                    if i >= 1:
                        sp.wait_ge(attn, i)
                    sp.dma_start(total_row, total_d[:, i % NT, :]).then_inc(total_in, 16)
                    if i % NT == TOP_ROWS_AT + 3 and 1 <= i // NT < HEADS - 1:
                        load_head_rows(i // NT + 1)
            with sp.Else():
                load_head_rows(2)
                load_head_rows(3)
            sp.wait_ge(head_out, HEADS)
            sp.dma_start(out.rearrange("(t p) f -> p t f", p=P), selfs[0:P]).then_inc(stored, 16)
            sp.wait_ge(stored, 16)


        @block.gpsimd
        def _(pool):
            pool.dma_start(att[:, 0, :], a["L0_gnn_att1"].rearrange("r b -> (r b)").partition_broadcast(128)).then_inc(att_in, 16)
            pool.dma_start(att[:, 1, :], a["L0_gnn_att2"].rearrange("r b -> (r b)").partition_broadcast(128)).then_inc(att_in, 16)
            pool.memset(ident[:, :], 0.0).then_inc(pool_step, 1)
            pool.memset(tri[:, :], 1.0).then_inc(pool_step, 1)
            pool.memset(ones_bf[:, :], 1.0).then_inc(const_ready, 1)
            pool.memset(ones_f, 1.0).then_inc(const_ready, 1)
            pool.memset(eps[:, :], LN_EPS).then_inc(const_ready, 1)
            pool.iota(iota_c[:, :], [[1, 128]], base=0, channel_multiplier=0,
                      allow_small_or_imprecise_dtypes=True).then_inc(const_ready, 1)
            pool.memset(table, -1.0).then_inc(pool_step, 1)
            pool.wait_ge(pool_step, 3)
            pool.affine_select(out=ident[:, :], in_=ident[:, :], compare_op=ALU.not_equal, fill=1.0,
                               base=0, pattern=[[-1, 128]], channel_multiplier=1).then_inc(const_ready, 1)
            pool.affine_select(out=tri[:, :], in_=tri[:, :], compare_op=ALU.is_gt, fill=0.0,
                               base=0, pattern=[[1, 128]], channel_multiplier=-1).then_inc(const_ready, 1)
            pool.dma_start(table_d.rearrange("(p j) f -> p j f", p=128), table).then_inc(table_clear, 16)

            def load_layer(l):
                if is_rgcn(l):
                    s = str(l + 1)
                    pool.dma_start(wts[:, 2], a["L0_gnn_root" + s].rearrange("(k p) f -> p k f", p=128)).then_inc(weights_in, 16)
                    pool.dma_start(bias[:, l % 2], a["L0_gnn_bias" + s].partition_broadcast(128)).then_inc(weights_in, 16)
                    for r in range(2):
                        with nc.allow_non_contiguous_dma(reason="512 gate weights"):
                            pool.dma_start(gate_w[:, l % 2, :, r], a["L0_gnn_gate_w" + s][r].rearrange("(k p) o -> p (k o)", p=128)).then_inc(weights_in, 16)
                elif is_conv(l):
                    s = str(l - CONV0 + 1)
                    pool.dma_start(wts[:, 0], a["L1_gnn_W1_" + s].rearrange("(k p) f -> p k f", p=128)).then_inc(weights_in, 16)
                    pool.dma_start(wts[:, 2], a["L1_gnn_W0_" + s].rearrange("(k p) f -> p k f", p=128)).then_inc(weights_in, 16)
                    pool.dma_start(bias[:, l % 2], a["L1_gnn_b" + s].partition_broadcast(128)).then_inc(weights_in, 16)
                elif is_sage(l):
                    pool.dma_start(wts[:, 0], a["L2_gnn_Ws_neigh"][l - SAGE0].rearrange("(k p) f -> p k f", p=128)).then_inc(weights_in, 16)
                    pool.dma_start(wts[:, 2], a["L2_gnn_Ws_self"][l - SAGE0].rearrange("(k p) f -> p k f", p=128)).then_inc(weights_in, 16)
                    pool.dma_start(bias[:, l % 2], a["L2_gnn_bs"][l - SAGE0].partition_broadcast(128)).then_inc(weights_in, 16)
                else:
                    for hd in range(HEADS):
                        pool.dma_start(wts[:, 0, :, hd * LAT:(hd + 1) * LAT],
                                       a["L3_gnn_W"][hd].rearrange("(k p) f -> p k f", p=128)).then_inc(weights_in, 16)

            def load_x(q, src):
                if q >= 2:
                    pool.wait_ge(x_ready, q - 1)
                    pool.wait_ge(x_stored[q % 2], 16 * ((q - 2) // 2 + 1))
                pool.dma_start(xin[0:P, q % 2], src).then_inc(x_in[q % 2], 16)

            load_layer(RGCN0)
            with nc.allow_non_contiguous_dma(reason="one scale per node"):
                pool.dma_start(node_scale[0:P, :], a["node_vec"].rearrange("(t p) -> p t", p=P)).then_inc(node_in, 16)
            pool.wait_ge(table_clear, 16)
            pool.wait_ge(slots_ready, 1)
            for c in range(EC):
                pool.indirect_dma_start(table_d, bass.IndirectOffsetOnAxis(slot[:, c:c + 1], 0), rec[:, c, :], None,
                                        bounds_check=SLOTS - 1, oob_is_err=False).then_inc(scattered, 16)
            for l in LAYERS:
                wait_tiles(pool, NT * (l + 1))
                load_layer(l + 1)
                if l == SAGE2:
                    pool.wait_ge(split_done, splits_before(GAT))
                    for v in range(2):
                        pool.dma_start(a_both[:, v].rearrange("p (h f) -> p h f", h=HEADS),
                                       a["L3_gnn_a"][:, (1 - v) * LAT:(2 - v) * LAT].partition_broadcast(128)).then_inc(a_in, 16)
                if l in (RGCN1, CONV1, SAGE2):
                    blk = (RGCN1, CONV1, SAGE2).index(l)
                    if blk:
                        for n in range(2):
                            pool.wait_ge(x_stored[n], 16 * 5 * blk)

                    def load(t):
                        load_x(NT * blk + t, rows(a["x"] if blk == 0 else x_d[blk - 1], t))
                        if l == CONV1:
                            pool.dma_start(hin[0:P, t % 2], rows(hin_d, t)).then_inc(hin_in[t % 2], 16)

                    load(0)
                    load(1)
                    for t in range(NT):
                        q = NT * blk + t
                        pool.wait_ge(x_ready, q + 1)
                        pool.dma_start(rows(x_d[blk], t), xin[0:P, q % 2]).then_inc(x_stored[q % 2], 16)
                        if l == RGCN1:
                            pool.wait_ge(h_ready, NT * (l + 1) + t + 1)
                            pool.dma_start(rows(hin_d, t), h_all[0:P, t]).then_inc(hin_stored, 16)
                        if t + 2 < NT:
                            load(t + 2)
                    if l == RGCN1:
                        pool.wait_ge(hin_stored, 16 * NT)
            pool.wait_ge(x_stored[0], 16 * 15)
            pool.wait_ge(x_stored[1], 16 * 15)
            pool.dma_start(selfs[0:P], x_d[2].rearrange("(t p) f -> p t f", p=P)).then_inc(x3_in, 16)
            pool.wait_ge(agg_mm, agg_before(GAT))
            pool.memset(hh[:, :, :, LAT:LAT + 1], 1.0).then_inc(gat_in, 1)

        @block.tensor
        def _(pe):
            pe.wait_ge(const_ready, 6)

            def prefix_product():
                pe.wait_ge(totals_ready, 1)
                pe.matmul(ps[0:P, 4, 0:BUCKETS], lhsT=tri[0:P, 0:P], rhs=totals, start=True, stop=True)
                pe.matmul(ps[:, 4, 128:128 + BUCKETS], lhsT=ones_f[0:P, :], rhs=totals, start=True, stop=True).then_inc(prefix_ready, 1)

            for n in range(NBAS):
                kh, b = divmod(n, BASES)
                if n == BASES:
                    pe.wait_ge(combined_out, 1)
                pe.wait_ge(basis_in[n % 4], 16 * (n // 4 + 1))
                pe.wait_ge(diag_ready, n + 1)
                for r in range(2):
                    for k in range(2):
                        last = pe.matmul(ps[:, 2 * r + k, :], lhsT=diag[:, 2 * (n % 2) + r, :], rhs=basis_ring[:, n % 4, k, :],
                                         start=(b == 0), stop=(b == BASES - 1))
                last.then_inc(basis_used, 1)
                if n == 14:
                    prefix_product()

            def transpose_tile(l, t):
                g = NT * l + t
                pe.wait_ge(h_ready, g + 1)
                if g >= 2:
                    pe.wait_ge(hT_ready, g - 1)
                for k in range(KT):
                    last = pe.transpose(ps[:, g % 2, k * P:(k + 1) * P], h_all[0:P, t, k * 128:(k + 1) * 128], ident[0:P, 0:P])
                last.then_inc(transposed, 1)

            def product(bank, l, t, w):
                g = NT * l + t
                for k in range(KT):
                    last = pe.matmul(bank, lhsT=hT_tile(g)[:, k, :], rhs=w(k), start=(k == 0), stop=(k == KT - 1))
                return last

            def act_bank(q):
                if q >= 2:
                    pe.wait_ge(zact_out, q - 1)
                return ps[0:P, 2 + q % 2, :]

            def vec_bank(q):
                if q >= 2:
                    pe.wait_ge(zvec_out, q - 1)
                return ps[0:P, 4 + q % 2, :]

            def node_scores(t):
                g = NT * GAT + t
                if t == 0:
                    pe.wait_ge(score_w_ready, 4)
                    pe.wait_ge(zvec_out, z_before(GAT, vec_groups))
                if t == 4:
                    pe.wait_ge(agg_out, agg_before(GAT))
                for k in range(KT):
                    pe.matmul(ps[0:P, 4, 8 * t:8 * t + 8], lhsT=hT_tile(g)[:, k, :], rhs=score_w[:, k, :],
                              start=(k == 0), stop=(k == KT - 1))
                for k in range(KT):
                    last = pe.matmul(ps[0:8, 5 + t // 4, (t % 4) * P:(t % 4 + 1) * P], lhsT=score_w[:, k, :], rhs=hT_tile(g)[:, k, :],
                                     start=(k == 0), stop=(k == KT - 1))
                last.then_inc(score_mm, 1)

            def weight_products(l):
                pe.wait_ge(weights_in, 16 * loads_before(l + 1))
                if l == RGCN0:
                    pe.wait_ge(combined_out, 2)
                if l == RGCN1:
                    pe.wait_ge(w2_ready, 1)
                transpose_tile(l, 0)
                if l == GAT:
                    for t in range(NT):
                        if t + 1 < NT:
                            transpose_tile(l, t + 1)
                        pe.wait_ge(hT_ready, NT * l + t + 1)
                        node_scores(t)
                for t in range(NT):
                    if l != GAT:
                        if t + 1 < NT:
                            transpose_tile(l, t + 1)
                        pe.wait_ge(hT_ready, NT * l + t + 1)
                    qa = z_before(l, act_groups) + act_groups(l) * t
                    if is_rgcn(l):
                        product(act_bank(qa)[:, 0:2], l, t, lambda k: gate_w[:, l % 2, k, :]).then_inc(zact_mm, 1)
                        for r in range(2):
                            product(act_bank(qa + 1 + r), l, t, lambda k: wts[:, r, k, :]).then_inc(zact_mm, 1)
                    else:
                        last = product(act_bank(qa), l, t, lambda k: wts[:, 0, k, :])
                        last.then_inc(zact_mm, 1)
                    if l != GAT:
                        qv = z_before(l, vec_groups) + t
                        last = product(vec_bank(qv), l, t, lambda k: wts[:, 2, k, :])
                        last.then_inc(zvec_mm, 1)

            def aggregate(l):
                if is_rgcn(l) or is_sage(l):
                    pe.wait_ge(split_done, splits_before(l + 1))
                else:
                    pe.wait_ge(zact_out, z_before(l + 1, act_groups))
                if l == SAGE0:
                    pe.wait_ge(deg_out, 1)
                if not is_conv(l):
                    with pe.If(general != 0):
                        rels = 2 if is_rgcn(l) else 1
                        if l:
                            pe.wait_ge(agg_out, agg_before(l))
                        first = rest_before(l) + (NT if l == SAGE0 else 0)
                        for t in range(NT):
                            if rest_tiles_before(l) + t:
                                pe.wait_ge(rest_out, rest_tiles_before(l) + t)
                            for r in range(rels):
                                pe.wait_ge(rest_in, 16 * (first + t * rels + r + 1))
                                for k in range(NT):
                                    for s in range(3):
                                        last = pe.matmul(ps[0:P, 6, :], lhsT=rest_slab[:, k, :], rhs=parts[0:P, r, s, k, :],
                                                         start=(r == 0 and k == 0 and s == 0),
                                                         stop=(r == rels - 1 and k == NT - 1 and s == 2))
                                last.then_inc(rest_used, 1)
                        pe.wait_ge(rest_out, rest_tiles_before(l) + NT)
                for t in range(NT):
                    g = NT * l + t
                    if g >= 2:
                        pe.wait_ge(agg_out, g - 1)
                    bank = ps[0:P, 6 + g % 2, :]
                    if is_conv(l):
                        n = (l - CONV0) * NT + t
                        pe.wait_ge(slab_in[n % 4], 16 * (n // 4 + 1))
                        for k in range(NT):
                            last = pe.matmul(bank, lhsT=slab(n)[:, k * P:(k + 1) * P], rhs=zfull[0:P, k, :],
                                             start=(k == 0), stop=(k == NT - 1))
                    else:
                        rels = 2 if is_rgcn(l) else 1
                        for r in range(rels):
                            for k in range(NT):
                                lhsT = adj[0:P, r, k, t * P:(t + 1) * P] if is_rgcn(l) else adj[0:P, 0, t, k * P:(k + 1) * P]
                                for s in range(3):
                                    last = pe.matmul(bank, lhsT=lhsT, rhs=parts[0:P, r, s, k, :],
                                                     start=(r == 0 and k == 0 and s == 0),
                                                     stop=(r == rels - 1 and k == NT - 1 and s == 2))
                    last.then_inc(agg_mm, 1)

            weight_products(RGCN0)

            pe.wait_ge(zact_out, z_before(RGCN1, act_groups))
            pe.wait_ge(zvec_out, z_before(RGCN1, vec_groups))
            general = overflowed(pe)
            with pe.If(general == 0):
                for m in range(BUCKETS // 2):
                    pe.wait_ge(hot_ready, m + 1)
                    if m >= 4:
                        pe.wait_ge(pair_act, m - 3)
                    hots = pair_hot(m)[0]
                    for b in range(2):
                        for v, factors in enumerate((((1, 0), (5, 0)), ((5, 0),), ((0, 1),), ((0, 2), (0, 3), (0, 4)))):
                            for j in range(2):
                                for i, (left, right) in enumerate(factors):
                                    last = pe.matmul(ps[:, 2 * (m % 4) + b, v * P:(v + 1) * P], lhsT=hots[left][:, :, 2 * b + j],
                                                     rhs=hots[right][:, 0:P, 2 * b + j], start=(j == 0 and i == 0),
                                                     stop=(j == 1 and i == len(factors) - 1))
                    last.then_inc(hot_used, 1)
                pe.wait_ge(pair_act, BUCKETS // 2)
            with pe.Else():
                with pe.Fori(0, NT) as qd:
                    with pe.Fori(0, NT // 2) as qp:
                        pe.wait_ge(pair_typed, 5 * qd + qp + 1)
                        for bb in range(2):
                            def chunk(c, first, last_one):
                                pe.wait_ge(chunk_hot, (10 * qd + 2 * qp + bb) * EC + c + 2)
                                for v, (left, right) in enumerate((((1, 0), (0,)), ((0, 5), (0,)), ((0, 0), (1,)), ((0, 0), (2, 3, 4)))):
                                    for rr in right:
                                        last = pe.matmul(ps[:, bb, v * P:(v + 1) * P], lhsT=onehots[0:P, left[0], left[1], :],
                                                         rhs=onehots[0:P, 0, rr, 0:P], start=first and v == 0,
                                                         stop=last_one, skip_group_check=True)
                                last.then_inc(chunk_used, 1)

                            chunk(0, True, False)
                            with pe.Fori(1, EC - 1) as c:
                                chunk(c, False, False)
                            chunk(EC - 1, False, True)
                pe.wait_ge(pair_typed, BUCKETS // 2 + 1)

            aggregate(RGCN0)
            for l in LAYERS[1:]:
                weight_products(l)
                if l == SAGE0:
                    pe.wait_ge(count_in, 16)
                    pe.wait_ge(agg_out, agg_before(SAGE0))
                    for t in range(NT):
                        for k in range(NT):
                            last = pe.matmul(ps[0:P, 6, t:t + 1], lhsT=adj[0:P, 0, t, k * P:(k + 1) * P], rhs=ones_bf[0:P, 0:1],
                                             start=(k == 0), stop=(k == NT - 1))
                    last.then_inc(deg_mm, 1)
                    with pe.If(general != 0):
                        for t in range(NT):
                            pe.wait_ge(rest_in, 16 * (rest_before(l) + t + 1))
                            for k in range(NT):
                                last = pe.matmul(ps[0:P, 7, t:t + 1], lhsT=rest_slab[:, k, :], rhs=ones_bf[0:P, 0:1],
                                                 start=(k == 0), stop=(k == NT - 1))
                            last.then_inc(rest_used, 1)
                aggregate(l)
            weight_products(GAT)

            def transpose_tops(h):
                pe.wait_ge(top_ready, h + 1)
                pe.transpose(ps[0:2 * NT, top_bank(h), 256:256 + P], score2[0:P, h].rearrange("p v t -> p (v t)"),
                             ident[0:P, 0:P]).then_inc(top_transposed, 1)

            pe.wait_ge(zact_out, z_before(GAT + 1, act_groups))
            transpose_tops(0)
            transpose_tops(1)
            pe.wait_ge(gat_in, 1)
            for h in range(HEADS):
                pe.wait_ge(top_row, max(2, h + 1))
                for k in range(NT):
                    if k == TOP_ROWS_AT and 1 <= h < HEADS - 1:
                        pe.wait_ge(head_out, h)
                        transpose_tops(h + 1)
                    pe.wait_ge(attn, h * NT + k + 1)
                    if k == 0 and h >= 2:
                        pe.wait_ge(head_out, h - 1)
                    for t in range(NT):
                        last = pe.matmul(ps[0:P, 4 * (h % 2) + t // 3, (t % 3) * (LAT + 1):(t % 3 + 1) * (LAT + 1)],
                                         lhsT=attn_t[0:P, (h * NT + k) % 2, t * P:(t + 1) * P], rhs=hh[0:P, k, h, :],
                                         start=(k == 0 and t % 3 == 0), stop=(k == NT - 1), skip_group_check=True)
                    last.then_inc(attn_used, 1)

        @block.scalar
        def _(act):
            act.wait_ge(const_ready, 6)
            act.wait_ge(att_in, 32)

            def copy_half(kh):
                act.wait_ge(basis_used, BASES * (kh + 1))
                for r in range(2):
                    last = act.activation(wts[:, r, 2 * kh:2 * kh + 2, :], ps[:, 2 * r:2 * r + 2, :], ACT.Copy)
                last.then_inc(combined_out, 1)

            def std(q):
                act.wait_ge(var_ready, q + 1)
                act.activation(mv[0:P, 2:3], mv[0:P, 1:2], ACT.Sqrt, bias=eps[0:P, :]).then_inc(std_ready, 1)

            for n in range(NBAS):
                b = n % BASES
                if n >= 2:
                    act.wait_ge(basis_used, n - 1)
                if n == BASES:
                    copy_half(0)
                if n == FIRST_STD:
                    act.wait_ge(first_var, 1)
                    act.activation(first_mv[:, :, 2], first_mv[:, :, 1], ACT.Sqrt, bias=eps[0:P, :]).then_inc(first_std, 1)
                for r in range(2):
                    last = act.activation(diag[:, 2 * (n % 2) + r, :], ident[:, :], ACT.Copy,
                                          scale=att[:, 0, r * BASES + b:r * BASES + b + 1])
                last.then_inc(diag_ready, 1)
            copy_half(1)

            def copy_hT(l, t):
                g = NT * l + t
                act.wait_ge(transposed, g + 1)
                if g >= 2 and l != GAT:
                    wait_tiles(act, g - 1)
                act.activation(hT_tile(g).rearrange("p k c -> p (k c)"), ps[:, g % 2, 0:KT * P], ACT.Copy).then_inc(hT_ready, 1)

            def empty_groups(l):
                s = splits_before(l)
                if l != GAT:
                    copy_hT(l, 0)
                for t in range(NT):
                    if t + 1 < NT and l != GAT:
                        copy_hT(l, t + 1)
                    q = z_before(l, act_groups) + act_groups(l) * t
                    if is_rgcn(l):
                        act.wait_ge(zact_mm, q + 1)
                        act.activation(gates[0:P, t % 2, :], ps[0:P, 2 + q % 2, 0:2], ACT.Sigmoid).then_inc(zact_out, 1)
                        act.wait_ge(zact_out, q + 1)
                        q += 1
                    for r in range(2 if is_rgcn(l) else 1):
                        act.wait_ge(zact_mm, q + 1)
                        bank = ps[0:P, 2 + q % 2, :]
                        if is_conv(l):
                            act.activation(zfull[0:P, t, :], bank, ACT.Copy).then_inc(zact_out, 1)
                        elif l == GAT:
                            act.activation(hh[0:P, t, :, 0:LAT], bank.rearrange("p (h f) -> p h f", h=HEADS), ACT.Copy).then_inc(zact_out, 1)
                        else:
                            scale = gates[0:P, t % 2, r:r + 1] if is_rgcn(l) else 1.0
                            if s >= 2:
                                act.wait_ge(split_done, s - 1)
                            act.activation(zt[0:P, s % 2], bank, ACT.Copy, scale=scale)
                            act.activation(parts[0:P, r, 0, t, :], bank, ACT.Copy, scale=scale).then_inc(zact_out, 1)
                            s += 1
                        q += 1

            empty_groups(RGCN0)
            wait_tiles(act, NT)
            act.wait_ge(basis2_used, EARLY)
            act.activation(wts[:, 0:2].rearrange("p r k f -> p (r k f)"), early_sum.rearrange("p r k f -> p (r k f)"), ACT.Copy).then_inc(sum_moved, 1)

            def empty_pair(m):
                qd, qp = divmod(m, NT // 2)
                act.wait_ge(hot_used, m + 1)
                bank = 2 * m % 8

                def blk(v):
                    return ps[0:P, bank:bank + 2, v * P:(v + 1) * P]

                def typed(r):
                    return adj[0:P, r, qd, 2 * qp * P:2 * (qp + 1) * P].rearrange("p (n c) -> p n c", n=2)

                act.activation(typed(0), blk(0), ACT.Copy)
                act.activation(typed(1), blk(1), ACT.Copy, scale=-1.0).then_inc(pair_typed, 1)
                if qp == 0 and qd >= 2:
                    act.wait_ge(stage_out[qd % 2], 32 * (qd // 2))
                act.activation(stage_c[0:P, qd % 2, 2 * qp:2 * qp + 2, :], blk(2), ACT.Copy)
                act.activation(stage_w[0:P, qd % 2, 2 * qp:2 * qp + 2, :], blk(3), ACT.Copy).then_inc(pair_act, 1)

            general = overflowed(act)
            with act.If(general == 0):
                act.wait_ge(sum_moved, 1)
                for m in range(BUCKETS // 2):
                    empty_pair(m)

            for l in LAYERS[1:]:
                empty_groups(l)
                if l in (RGCN1, CONV1, SAGE2):
                    blk0 = NT * (RGCN1, CONV1, SAGE2).index(l)
                    for t in range(NT):
                        std(blk0 + t)
            for t in range(NT):
                copy_hT(GAT, t)
            act.wait_ge(score_mm, NT)
            act.activation(score_rows[:, 0:8 * P].rearrange("p (n c) -> p n c", n=2), ps[0:8, 5:7, 0:4 * P], ACT.Copy)
            act.activation(score_rows[:, 8 * P:NODES], ps[0:8, 7, 0:2 * P], ACT.Copy).then_inc(score_row, 1)
            empty_groups(GAT)

            def copy_top_rows(h):
                act.wait_ge(top_transposed, h + 1)
                if h >= 2:
                    act.wait_ge(rows_stored, 16 * h)
                act.activation(top_rows[:, h % 2, :], ps[0:2 * NT, top_bank(h), 256:256 + P], ACT.Copy).then_inc(top_row, 1)

            def below_pos(i):
                h, k = divmod(i, NT)
                if k == 0:
                    act.wait_ge(headrow_in[h % 2], 32 * (h // 2 + 1))
                if i >= 3:
                    act.wait_ge(attn, i - 2)
                if not vector_neg(i):
                    act.activation(neg_t[0:P, i % 2], head_rows[0:P, h % 2, 1, :], ACT.Relu, bias=minus_slope_dst[0:P, k, h:h + 1])
                act.activation(pos_t[0:P, i % 3], head_rows[0:P, h % 2, 0, :], ACT.Relu, bias=minus_dst[0:P, k, h:h + 1]).then_inc(pos_ready, 1)

            copy_top_rows(0)
            copy_top_rows(1)
            below_pos(0)
            below_pos(1)
            for i in range(HEADS * NT):
                act.wait_ge(below, i + 1)
                act.activation(pos_t[0:P, i % 3], pos_t[0:P, i % 3], ACT.Exp, scale=-1.0).then_inc(expd, 1)
                if i + 2 < HEADS * NT:
                    below_pos(i + 2)
                if i % NT == TOP_ROWS_AT and 1 <= i // NT < HEADS - 1:
                    copy_top_rows(i // NT + 1)

        @block.vector
        def _(dve):
            steps = [0]

            def step(ins):
                steps[0] += 1
                ins.then_inc(dve_step, 1)
                dve.wait_ge(dve_step, steps[0])

            dve.wait_ge(const_ready, 6)
            dve.wait_ge(edge_in, 64)
            sd, quo, low = rk[0:P, 640:960], rk[0:P, 960:1280], rk[0:P, 1280:1600]
            dve.tensor_copy(sd, rk[0:P, 0:320].bitcast(I32))
            step(dve.tensor_scalar(rec[:, :, 2], rk[0:P, 320:480].bitcast(I32), 0, None, ALU.not_equal))
            step(dve.tensor_scalar(quo, sd, float(P), None, ALU.is_ge))
            for k in range(2, NT):
                step(dve.scalar_tensor_tensor(quo, sd, float(k * P), quo, ALU.is_ge, ALU.add))
            step(dve.scalar_tensor_tensor(low, quo, -float(P), sd, ALU.mult, ALU.add))
            dve.tensor_copy(rec[:, :, 0], low[:, 0:EC])
            dve.tensor_copy(rec[:, :, 1], low[:, EC:2 * EC])
            dve.tensor_copy(rec[:, :, 3], rk[0:P, 480:640])
            step(dve.scalar_tensor_tensor(bucket, quo[:, EC:2 * EC], float(NT), quo[:, 0:EC], ALU.mult, ALU.add))
            for b in range(BUCKETS):
                last = dve.tensor_scalar(hot[:, b, :], bucket, float(b), 0.0, ALU.is_equal, ALU.add, accum_out=totals[:, b:b + 1])
            last.then_inc(totals_ready, 1)
            dve.wait_ge(prefix_ready, 1)
            dve.tensor_copy(before, ps[0:P, 4, 0:BUCKETS])
            step(dve.tensor_reduce(fullest[:, :], ps[:, 4, 128:128 + BUCKETS], AX.X, ALU.max))
            dve.tensor_scalar(overflow[:, :], fullest[:, :], CAP + 0.5, None, ALU.is_ge).then_inc(overflow_ready, 1)
            for b in range(BUCKETS):
                last = dve.tensor_tensor_scan(running[:, b, :], ones_bf[0:P, :], hot[:, b, :], before[:, b:b + 1], ALU.mult, ALU.add)
            step(last)
            step(dve.tensor_tensor(running, running, hot, ALU.mult))
            step(dve.tensor_reduce(rank, running.rearrange("p b c -> p c b"), AX.X, ALU.add))
            step(dve.tensor_scalar(high, rank, 128.5, -float(128 * CHUNKS - 1), ALU.is_ge, ALU.mult))
            step(dve.scalar_tensor_tensor(high, bucket, 2.0, high, ALU.mult, ALU.add))
            step(dve.tensor_scalar(rank, rank, -1.0, float(CHUNKS), ALU.add, ALU.mult))
            step(dve.tensor_tensor(rank, rank, high, ALU.add))
            dve.tensor_copy(slot, rank).then_inc(slots_ready, 1)

            def norm_relu(q, xt, ht):
                step(dve.bn_stats(stats[0:P, :], xt))
                dve.bn_aggr(mv[0:P, 0:2], stats[0:P, :]).then_inc(var_ready, 1)
                dve.wait_ge(std_ready, q + 1)
                step(dve.reciprocal(mv[0:P, 3:4], mv[0:P, 2:3]))
                step(dve.tensor_scalar(ht, xt, mv[0:P, 0:1], mv[0:P, 3:4], ALU.subtract, ALU.mult))
                dve.tensor_scalar(ht, ht, 0.0, None, ALU.max).then_inc(h_ready, 1)

            def sum_basis2(n, sums):
                b, kh = divmod(n, 2)
                dve.wait_ge(basis2_in[n % 4], 16 * (n // 4 + 1))
                if n >= 2:
                    dve.wait_ge(basis2_used, n - 1)
                half = early_ring[:, n % 4] if n < EARLY else basis2_ring[:, n % 2]
                for r in range(2):
                    w = sums[:, r, 2 * kh:2 * kh + 2, :]
                    coef = att[:, 1, r * BASES + b:r * BASES + b + 1]
                    if b == 0:
                        last = dve.tensor_scalar(w, half, coef, None, ALU.mult)
                    else:
                        last = dve.scalar_tensor_tensor(w, half, coef, w, ALU.mult, ALU.add)
                last.then_inc(basis2_used, 1)

            dve.wait_ge(first_x_in, 16)
            for t in range(NT):
                last = dve.bn_stats(first_stats[:, t, :], h_all[0:P, t])
            step(last)
            for t in range(NT):
                last = dve.bn_aggr(first_mv[:, t, 0:2], first_stats[:, t, :])
            last.then_inc(first_var, 1)
            dve.wait_ge(att_in, 32)
            for n in range(6):
                sum_basis2(n, early_sum)
            dve.wait_ge(first_std, 1)
            step(dve.reciprocal(first_mv[:, :, 3], first_mv[:, :, 2]))
            for t in range(NT):
                last = dve.tensor_scalar(h_all[0:P, t], h_all[0:P, t], first_mv[:, t, 0:1], first_mv[:, t, 3:4], ALU.subtract, ALU.mult)
            step(last)
            for t in range(NT):
                dve.tensor_scalar(h_all[0:P, t], h_all[0:P, t], 0.0, None, ALU.max).then_inc(h_ready, 1)
            summed = [BEFORE_Z]
            for n in range(6, BEFORE_Z):
                sum_basis2(n, early_sum)

            def one_more(l):
                if l == RGCN0 and summed[0] < EARLY:
                    sum_basis2(summed[0], early_sum)
                    summed[0] += 1

            dve.wait_ge(node_in, 16)

            def self_terms_and_splits(l):
                s = splits_before(l)
                dve.wait_ge(weights_in, 16 * loads_before(l + 1))
                for t in range(NT):
                    q = z_before(l, act_groups) + act_groups(l) * t
                    for r in range(0 if is_conv(l) else 2 if is_rgcn(l) else 1):
                        dve.wait_ge(zact_out, q + (2 if is_rgcn(l) else 1) + r)
                        step(dve.tensor_tensor(zt[0:P, s % 2], zt[0:P, s % 2], parts[0:P, r, 0, t, :], ALU.subtract))
                        step(dve.tensor_copy(parts[0:P, r, 1, t, :], zt[0:P, s % 2]))
                        dve.tensor_tensor(parts[0:P, r, 2, t, :], zt[0:P, s % 2], parts[0:P, r, 1, t, :], ALU.subtract).then_inc(split_done, 1)
                        s += 1
                        one_more(l)
                    qv = z_before(l, vec_groups) + t
                    dve.wait_ge(zvec_mm, qv + 1)
                    bank = ps[0:P, 4 + qv % 2, :]
                    if is_conv(l):
                        dve.scalar_tensor_tensor(selfs[0:P, t], bank, node_scale[0:P, t:t + 1], bias[0:P, l % 2, :],
                                                 ALU.mult, ALU.add).then_inc(zvec_out, 1)
                    else:
                        dve.tensor_tensor(selfs[0:P, t], bank, bias[0:P, l % 2, :], ALU.add).then_inc(zvec_out, 1)
                    one_more(l)

            def epilogue(l, t):
                g = NT * l + t
                dve.wait_ge(agg_mm, g + 1)
                bank = ps[0:P, 6 + g % 2, :]
                tmp = ht_tmp[0:P, t % 2]
                if is_sage(l):
                    ins = dve.scalar_tensor_tensor(tmp, bank, inv_deg[0:P, t:t + 1], selfs[0:P, t], ALU.mult, ALU.add)
                else:
                    ins = dve.tensor_tensor(tmp, bank, selfs[0:P, t], ALU.add)
                ins.then_inc(agg_out, 1)
                dve.wait_ge(agg_out, g + 1)
                if l in (RGCN0, CONV0, SAGE0, SAGE1):
                    dve.tensor_scalar(h_all[0:P, t], tmp, 0.0, None, ALU.max).then_inc(h_ready, 1)
                    return
                q = NT * (RGCN1, CONV1, SAGE2).index(l) + t
                x = xin[0:P, q % 2]
                dve.wait_ge(x_in[q % 2], 16 * (q // 2 + 1))
                if l == CONV1:
                    dve.wait_ge(hin_in[t % 2], 16 * (t // 2 + 1))
                    step(dve.scalar_tensor_tensor(tmp, tmp, 0.0, hin[0:P, t % 2], ALU.max, ALU.add))
                    step(dve.scalar_tensor_tensor(x, tmp, 0.5, x, ALU.mult, ALU.add))
                else:
                    step(dve.tensor_tensor(x, x, tmp, ALU.add))
                norm_relu(q, x, h_all[0:P, t])
                dve.engine_nop().then_inc(x_ready, 1)

            def add_rests(l):
                if is_conv(l):
                    return
                rels = 2 if is_rgcn(l) else 1
                first = rest_before(l) + (NT if l == SAGE0 else 0)
                with dve.If(general != 0):
                    for t in range(NT):
                        dve.wait_ge(rest_used, first + (t + 1) * rels)
                        if is_sage(l):
                            dve.scalar_tensor_tensor(selfs[0:P, t], ps[0:P, 6, :], inv_deg[0:P, t:t + 1], selfs[0:P, t], ALU.mult, ALU.add).then_inc(rest_out, 1)
                        else:
                            dve.tensor_tensor(selfs[0:P, t], ps[0:P, 6, :], selfs[0:P, t], ALU.add).then_inc(rest_out, 1)
                    dve.wait_ge(rest_out, rest_tiles_before(l) + NT)

            self_terms_and_splits(RGCN0)

            def all_edges():
                dve.wait_ge(raw_ready, 64)
                started = [0]

                def first(ins):
                    started[0] += 1
                    ins.then_inc(raw_step, 1)
                    dve.wait_ge(raw_step, started[0])

                wbf, wrest = ht_tmp[0:P, 0, 0:EC // 2].bitcast(BF16), ht_tmp[0:P, 1, 0:EC]
                w = raw_in[:, 3 * EC:]
                first(dve.tensor_copy(raw_node.rearrange("p v c -> p (v c)"), raw_in[:, 0:2 * EC].bitcast(I32)))
                first(dve.tensor_scalar(raw_type[:, 0, :], raw_in[:, 2 * EC:3 * EC].bitcast(I32), 0, None, ALU.is_equal))
                first(dve.tensor_scalar(raw_type[:, 1, :], raw_in[:, 2 * EC:3 * EC].bitcast(I32), 0, None, ALU.not_equal))
                first(dve.tensor_scalar(tile_base, iota_c[0:P, 0:NT], float(P), None, ALU.mult))
                first(dve.tensor_copy(wbf, w))
                first(dve.tensor_copy(raw_w[:, 0, :], wbf))
                first(dve.tensor_tensor(wrest, w, raw_w[:, 0, :], ALU.subtract))
                first(dve.tensor_copy(wbf, wrest))
                first(dve.tensor_copy(raw_w[:, 1, :], wbf))
                first(dve.tensor_tensor(raw_w[:, 2, :], wrest, raw_w[:, 1, :], ALU.subtract))
                per_pair = 4 + 3 * 2 + 1
                dve.engine_nop().then_inc(chunk_hot, 1)
                dve.engine_nop().then_inc(chunk_used, 1)
                dve.engine_nop().then_inc(pair_typed, 1)
                with dve.Fori(0, NT) as qd:
                    with dve.Fori(0, NT // 2) as qp:
                        done = [0]

                        def mark(ins):
                            done[0] += 1
                            ins.then_inc(raw_step, 1)

                        def wait_marks():
                            dve.wait_ge(raw_step, started[0] + (5 * qd + qp) * per_pair + done[0])

                        for bb in range(2):
                            dve.wait_ge(chunk_hot, (10 * qd + 2 * qp + bb) * EC + 1)
                            mark(dve.tensor_scalar(rel_node[:, 0, :], raw_node[:, 0, :], tile_base[:, bass.ds(2 * qp + bb, 1)], None, ALU.subtract))
                            mark(dve.tensor_scalar(rel_node[:, 1, :], raw_node[:, 1, :], tile_base[:, bass.ds(qd, 1)], None, ALU.subtract))
                            with dve.Fori(0, EC) as c:
                                wait_marks()
                                dve.wait_ge(chunk_used, (10 * qd + 2 * qp + bb) * EC + c + 1)
                                src, dst = rel_node[:, 0, bass.ds(c, 1)], rel_node[:, 1, bass.ds(c, 1)]
                                dve.tensor_scalar(onehots[0:P, 0, 0, :], iota_c[0:P, :], src, None, ALU.is_equal)
                                dve.tensor_scalar(onehots[0:P, 0, 1, :], iota_c[0:P, :], dst, None, ALU.is_equal)
                                for s in range(3):
                                    dve.tensor_scalar(onehots[0:P, 0, 2 + s, :], iota_c[0:P, :], dst, raw_w[:, s, bass.ds(c, 1)], ALU.is_equal, ALU.mult)
                                dve.tensor_scalar(onehots[0:P, 0, 5, :], iota_c[0:P, :], dst, raw_type[:, 1, bass.ds(c, 1)], ALU.is_equal, ALU.mult)
                                dve.tensor_scalar(onehots[0:P, 1, 0, :], iota_c[0:P, :], dst, raw_type[:, 0, bass.ds(c, 1)], ALU.is_equal, ALU.mult).then_inc(chunk_hot, 1)
                        dve.wait_ge(chunk_used, (10 * qd + 2 * qp + 2) * EC + 1)

                        def blk(v):
                            return ps[0:P, 0:2, v * P:(v + 1) * P]

                        def cols(ap):
                            return ap[:, bass.ds(qp * (2 * P), 2 * P)].rearrange("p (n c) -> p n c", n=2)

                        total = cols(stage_w[0:P, 1].rearrange("p k c -> p (k c)"))
                        for v in range(3):
                            if v < 2:
                                near = cols(adj[0:P, v, bass.ds(qd, 1), :].rearrange("p o n -> p (o n)"))
                                rest = cols(rest_row[:, v, :])
                            else:
                                near = cols(stage_c[0:P, 0].rearrange("p k c -> p (k c)"))
                                rest = cols(stage_c[0:P, 1].rearrange("p k c -> p (k c)"))
                            mark(dve.tensor_copy(near, blk(v)))
                            wait_marks()
                            mark(dve.tensor_tensor(rest, blk(v), near, ALU.subtract))
                        mark(dve.tensor_copy(total, blk(0)))
                        wait_marks()
                        dve.tensor_tensor(total, total, blk(1), ALU.add)
                        dve.tensor_copy(cols(stage_w[0:P, 0].rearrange("p k c -> p (k c)")), blk(3)).then_inc(pair_typed, 1)
                    dve.wait_ge(row_stored, 96 * qd + 96)

            general = overflowed(dve)
            steps_before = steps[0]
            with dve.If(general == 0):
                dve.wait_ge(table_in, 16)
                dve.tensor_copy(iota4, iota_c[:, :].unsqueeze(2).broadcast_to([128, 128, 4]))
                dve.tensor_copy(node_bf, table[:, :, 0:2].rearrange("p j v -> p v j"))
                dve.tensor_scalar(coef_bf[:, 3, :], table[:, :, 2], -1.0, None, ALU.mult)
                wrest = ht_tmp[:, 0, 0:CHUNKS]
                step(dve.tensor_copy(coef_bf[:, 0, :], table[:, :, 3]))
                step(dve.tensor_tensor(wrest, table[:, :, 3], coef_bf[:, 0, :], ALU.subtract))
                step(dve.tensor_copy(coef_bf[:, 1, :], wrest))
                step(dve.tensor_tensor(coef_bf[:, 2, :], wrest, coef_bf[:, 1, :], ALU.subtract))
                for m in range(BUCKETS // 2 + 1):
                    if m < BUCKETS // 2:
                        if m >= 3:
                            dve.wait_ge(hot_used, m - 2)
                        dve.tensor_tensor(pair_hot(m)[1], iota4.unsqueeze(1).broadcast_to([128, 2, 128, 4]),
                                          node_bf[:, :, 4 * m:4 * m + 4].unsqueeze(2).broadcast_to([128, 2, 128, 4]), ALU.is_equal).then_inc(nodes_hot, 1)
                    if m >= 1:
                        of, _, coefs = pair_hot(m - 1)
                        dve.wait_ge(nodes_hot, m)
                        dve.tensor_tensor(coefs, of[1].unsqueeze(1).broadcast_to([128, 4, 128, 4]),
                                          coef_bf[:, :, 4 * m - 4:4 * m].unsqueeze(2).broadcast_to([128, 4, 128, 4]), ALU.mult).then_inc(hot_ready, 1)
                for n in range(2):
                    dve.wait_ge(stage_out[n], 16 * NT)
            with dve.Else():
                dve.engine_nop().then_inc(dve_step, steps[0] - steps_before)
                dve.wait_ge(sum_moved, 1)
                all_edges()

            add_rests(RGCN0)
            wait_tiles(dve, NT)
            for t in range(NT):
                for n in range(EARLY + (NBAS - EARLY) * t // NT, EARLY + (NBAS - EARLY) * (t + 1) // NT):
                    sum_basis2(n, wts)
                epilogue(RGCN0, t)
            dve.wait_ge(basis2_used, 2 * BASES)
            dve.engine_nop().then_inc(w2_ready, 1)

            def score_weights(n):
                v, kp = divmod(n, 2)
                if n == 0:
                    dve.wait_ge(weights_in, 16 * loads_before(GAT + 1))
                    dve.wait_ge(a_in, 32)
                prod = hin[:, :, :]
                step(dve.tensor_tensor(prod, wts[:, 0, 2 * kp:2 * kp + 2, :], a_both[:, v:v + 1, :].broadcast_to([128, 2, H]), ALU.mult))
                step(dve.tensor_reduce(score_w[:, 2 * kp:2 * kp + 2, 4 * v:4 * v + 4], prod.rearrange("p k (h f) -> p k h f", h=HEADS), AX.X, ALU.add))
                dve.engine_nop().then_inc(score_w_ready, 1)

            for l in LAYERS[1:]:
                self_terms_and_splits(l)
                if l == CONV0:
                    dve.wait_ge(hin_stored, 16 * NT)
                if l == SAGE0:
                    dve.wait_ge(deg_mm, 1)
                    step(dve.tensor_copy(inv_deg[0:P, :], ps[0:P, 6, 0:NT]))
                    with dve.If(general != 0):
                        dve.wait_ge(rest_used, rest_before(l) + NT)
                        dve.tensor_tensor(inv_deg[0:P, :], inv_deg[0:P, :], ps[0:P, 7, 0:NT], ALU.add).then_inc(rest_degree, 1)
                        dve.wait_ge(rest_degree, 1)
                    step(dve.tensor_scalar(inv_deg[0:P, :], inv_deg[0:P, :], 1.0, None, ALU.max))
                    dve.reciprocal(inv_deg[0:P, :], inv_deg[0:P, :]).then_inc(deg_out, 1)
                    dve.wait_ge(deg_out, 1)
                add_rests(l)
                for t in range(NT):
                    epilogue(l, t)
                    if l == SAGE2 and 1 <= t <= 4:
                        score_weights(t - 1)
                if l == SAGE1:
                    dve.wait_ge(typed_in, 32)
                    dve.tensor_tensor(adj[0:P, 1], adj[0:P, 1], type1_in, ALU.add).then_inc(gat_typed, 1)

            step(dve.tensor_scalar(adj[0:P, 0], adj[0:P, 0], 0.0, NEG, ALU.is_equal, ALU.mult))
            dve.wait_ge(score_mm, NT)
            step(dve.tensor_copy(score[0:P].rearrange("p t v -> p (t v)"), ps[0:P, 4, 0:8 * NT]))
            dve.tensor_scalar(minus_dst[0:P], score[0:P, :, 0:4], -1.0, None, ALU.mult)
            dve.tensor_scalar(minus_slope_dst[0:P], score[0:P, :, 0:4], -SLOPE, None, ALU.mult)

            def tile_top(h, t):
                step(dve.tensor_tensor_reduce(max_t, adj[0:P, 0, :, t * P:(t + 1) * P], ad_rows[0:P, h, :].rearrange("p (k c) -> p k c", k=NT),
                                              1.0, NEG, ALU.add, ALU.max, top[0:P, h, t:t + 1]))

            def finish_tops(h):
                src = score[0:P, :, 4 + h]
                step(dve.tensor_tensor(top[0:P, h], top[0:P, h], src, ALU.add))
                step(dve.scalar_tensor_tensor(top[0:P, h], top[0:P, h], SLOPE, top[0:P, h], ALU.mult, ALU.max))
                dve.tensor_tensor(score2[0:P, h, 0], top[0:P, h], src, ALU.subtract)
                dve.scalar_tensor_tensor(score2[0:P, h, 1], src, -SLOPE, top[0:P, h], ALU.mult, ALU.add).then_inc(top_ready, 1)

            dve.wait_ge(adrow_in, 16 * HEADS)
            for h in range(2):
                for t in range(NT):
                    tile_top(h, t)
                finish_tops(h)

            def finish_head(h):
                dve.wait_ge(attn_used, NT * (h + 1))
                b0 = 4 * (h % 2)
                den = ps[0:P, b0:b0 + 3, 0:3 * (LAT + 1)].rearrange("p n (c f) -> p n c f", c=3)[:, :, :, LAT]
                step(dve.tensor_scalar(rden[0:P, 0:9].rearrange("p (n c) -> p n c", n=3), den, 1e-30, None, ALU.max))
                step(dve.tensor_scalar(rden[0:P, 9:10], ps[0:P, b0 + 3, LAT:LAT + 1], 1e-30, None, ALU.max))
                step(dve.reciprocal(rden[0:P], rden[0:P]))
                for t in range(NT):
                    c0 = (t % 3) * (LAT + 1)
                    x = selfs[0:P, t, h * LAT:(h + 1) * LAT]
                    last = dve.scalar_tensor_tensor(x, ps[0:P, b0 + t // 3, c0:c0 + LAT], rden[0:P, t:t + 1], x, ALU.mult, ALU.add)
                last.then_inc(head_out, 1)

            dve.wait_ge(gat_typed, 1)
            dve.wait_ge(x3_in, 16)
            def smaller(i):
                h, k = divmod(i, NT)
                if vector_neg(i):
                    dve.tensor_scalar(neg_vec, head_rows[0:P, h % 2, 1, :], minus_slope_dst[0:P, k, h:h + 1], 0.0,
                                      ALU.add, ALU.max).then_inc(neg_ready, 1)
                    dve.wait_ge(neg_ready, sum(vector_neg(j) for j in range(i + 1)))
                dve.wait_ge(pos_ready, i + 1)
                neg = neg_vec if vector_neg(i) else neg_t[0:P, i % 2]
                dve.tensor_tensor(pos_t[0:P, i % 3], pos_t[0:P, i % 3], neg, ALU.min).then_inc(below, 1)

            def attention(count, ready):
                smaller(0)
                for i in range(HEADS * NT):
                    if i + 1 < HEADS * NT:
                        smaller(i + 1)
                    dve.wait_ge(expd, i + 1)
                    if i >= 2:
                        dve.wait_ge(attn_used, i - 1)
                    ready(i)
                    dve.tensor_tensor(attn_t[0:P, i % 2], pos_t[0:P, i % 3], count(i), ALU.mult).then_inc(attn, 1)
                    if i % NT == 1 and i > NT:
                        finish_head(i // NT - 1)
                    if i // NT + 2 < HEADS:
                        tile_top(i // NT + 2, i % NT)
                        if i % NT == NT - 1:
                            finish_tops(i // NT + 2)
                finish_head(HEADS - 1)

            steps_before = steps[0]
            with dve.If(general == 0):
                attention(lambda i: adj[0:P, 1, i % NT, :], lambda i: None)
            with dve.Else():
                steps[0] = steps_before
                attention(lambda i: total_row, lambda i: dve.wait_ge(total_in, 16 * (i + 1)))


_INS = ["x", "src", "dst", "edge_type_2", "edge_weight", "node_vec",
        "L0_gnn_basis1", "L0_gnn_att1", "L0_gnn_gate_w1", "L0_gnn_root1", "L0_gnn_bias1",
        "L0_gnn_basis2", "L0_gnn_att2", "L0_gnn_gate_w2", "L0_gnn_root2", "L0_gnn_bias2",
        "L1_gnn_W0_1", "L1_gnn_W1_1", "L1_gnn_b1", "L1_gnn_W0_2", "L1_gnn_W1_2", "L1_gnn_b2",
        "L2_gnn_Ws_self", "L2_gnn_Ws_neigh", "L2_gnn_bs", "L3_gnn_W", "L3_gnn_a"]


def kernel(**inputs):
    import concourse.bacc as bacc
    from concourse.bass_utils import run_bass_kernel_spmd as run

    nc = bacc.Bacc("TRN2", target_bir_lowering=False, num_devices=1)
    arrays, args = {}, {}
    for name in _INS:
        arr = np.ascontiguousarray(inputs[name])
        arrays[f"in_{name}"] = arr
        args[name] = nc.dram_tensor(f"in_{name}", arr.shape, mybir.dt.from_np(arr.dtype), kind="ExternalInput").ap()
    out = nc.dram_tensor("out_x", (NODES, H), F32, kind="ExternalOutput").ap()
    build(nc, args, out)
    r = run(nc, [arrays], core_ids=[0])
    return r.results[0]["out_x"]
```
